# Optimizing a Trainium2 kernel written in Bass

```python
import numpy as np
import jax
import jax.numpy as jnp

def _softmax(x, axis=-1):
    return jax.nn.softmax(x, axis=axis)

def _gelu(x):
    return jax.nn.gelu(x, approximate=True)

def _silu(x):
    return jax.nn.silu(x)

def _sigmoid(x):
    return jax.nn.sigmoid(x)

def _layernorm(x, axis=-1, eps=1e-05):
    m = jnp.mean(x, axis=axis, keepdims=True)
    v = jnp.var(x, axis=axis, keepdims=True)
    return (x - m) / jnp.sqrt(v + eps)

def _scatter_add(tgt, idx, src, axis=0):
    return tgt.at[idx].add(src)

def _segment_sum(src, seg, n):
    return jax.ops.segment_sum(src, seg, n)
kernel_name = 'mk_sandwich_d2_jaxref_r8_bdd931'

def setup_inputs(seed: int=0):
    np.random.seed(seed)
    _w = jnp.asarray

    def _L0_attn_setup():
        import jax, jax.numpy as jnp
        import numpy as np
        B, L, D = (4, 512, 128)
        PHAZOR_SCALE_START = 32.0
        PHAZOR_SCALE_END = 2048.0
        key = jax.random.key(seed)
        ks = jax.random.split(key, 7)
        x = jax.random.normal(ks[0], (B, L, D), dtype=jnp.float32)
        phazor_init_re = jax.random.normal(ks[1], (D,), dtype=jnp.float32)
        phazor_init_im = jax.random.normal(ks[2], (D,), dtype=jnp.float32)
        phazor_angle = jax.random.normal(ks[3], (D,), dtype=jnp.float32)
        ln_minus_ln_phazor_abs = jax.random.normal(ks[4], (D,), dtype=jnp.float32)
        last_conv_re = jax.random.normal(ks[5], (D,), dtype=jnp.float32)
        last_conv_im = jax.random.normal(ks[6], (D,), dtype=jnp.float32)
        ln_phazor_scale = jnp.exp(jnp.linspace(np.log(1.0 / PHAZOR_SCALE_START), np.log(1.0 / PHAZOR_SCALE_END), D)).astype(jnp.float32)
        return {'x': x, 'phazor_init_re': phazor_init_re, 'phazor_init_im': phazor_init_im, 'phazor_angle': phazor_angle, 'ln_minus_ln_phazor_abs': ln_minus_ln_phazor_abs, 'last_conv_re': last_conv_re, 'last_conv_im': last_conv_im, 'ln_phazor_scale': ln_phazor_scale}
    _L0_attn_in = _L0_attn_setup()

    def _L0_ffn_setup():
        import jax, jax.numpy as jnp
        import numpy as np
        TOP_K = 2
        NUM_EXPERTS = 8
        key = jax.random.key(seed)
        ks = jax.random.split(key, 8)
        h, d, ds, E = (128, 64, 128, NUM_EXPERTS)
        s = 1.0 / np.sqrt(h)
        return {'x': jax.random.normal(ks[0], (2, 256, h), jnp.float32), 'router': jax.random.normal(ks[1], (h, E), jnp.float32) * s, 'experts_gate': jax.random.normal(ks[2], (E, h, d), jnp.float32) * s, 'experts_up': jax.random.normal(ks[3], (E, h, d), jnp.float32) * s, 'experts_down': jax.random.normal(ks[4], (E, d, h), jnp.float32) * (1.0 / np.sqrt(d)), 'shared_gate': jax.random.normal(ks[5], (h, ds), jnp.float32) * s, 'shared_up': jax.random.normal(ks[6], (h, ds), jnp.float32) * s, 'shared_down': jax.random.normal(ks[7], (ds, h), jnp.float32) * (1.0 / np.sqrt(ds))}
    _L0_ffn_in = _L0_ffn_setup()

    def _L1_attn_setup():
        import math
        import jax, jax.numpy as jnp
        import numpy as np
        HEADS = 16
        DIM_HEAD = 64
        NUM_NULL_KV = 2
        ATTN_SCALE = 8.0
        LN_EPS = 1e-05

        def _alibi_slopes(heads):
            start = 2.0 ** (-2.0 ** (-(math.log2(heads) - 3.0)))
            return np.array([start * start ** i for i in range(heads)], dtype=np.float32)

        def _l2norm(t):
            return t / jnp.maximum(jnp.linalg.norm(t, axis=-1, keepdims=True), 1e-12)
        key = jax.random.key(seed)
        ks = jax.random.split(key, 5)
        b, n, dim = (4, 256, 128)
        return {'x': jax.random.normal(ks[0], (b, n, dim), dtype=jnp.float32), 'gamma': jnp.ones((dim,), dtype=jnp.float32), 'w_q': jax.random.normal(ks[1], (dim, HEADS * DIM_HEAD), dtype=jnp.float32) * 0.02, 'w_kv': jax.random.normal(ks[2], (dim, 2 * HEADS * DIM_HEAD), dtype=jnp.float32) * 0.02, 'null_kv': jax.random.normal(ks[3], (HEADS, 2 * NUM_NULL_KV, DIM_HEAD), dtype=jnp.float32), 'q_scale': jnp.ones((DIM_HEAD,), dtype=jnp.float32), 'k_scale': jnp.ones((DIM_HEAD,), dtype=jnp.float32), 'w_out': jax.random.normal(ks[4], (HEADS * DIM_HEAD, dim), dtype=jnp.float32) * 0.02}
    _L1_attn_in = _L1_attn_setup()

    def _L1_ffn_setup():
        import jax, jax.numpy as jnp
        import numpy as np
        B, S, H, I, E, K = (4, 256, 128, 512, 4, 2)

        def _layer_norm(h, g, b, eps=1e-05):
            mu = h.mean(-1, keepdims=True)
            var = ((h - mu) ** 2).mean(-1, keepdims=True)
            return (h - mu) * jax.lax.rsqrt(var + eps) * g + b
        key = jax.random.key(seed)
        ks = jax.random.split(key, 24)
        rn = lambda k, shape, s=0.02: jax.random.normal(k, shape, dtype=jnp.float32) * s
        z = lambda shape: jnp.zeros(shape, jnp.float32)
        o = lambda shape: jnp.ones(shape, jnp.float32)
        return {'x': rn(ks[0], (B, S, H), 1.0), 'router_w': rn(ks[1], (H, E)), 'router_b': z((E,)), 'load_balancer': o((E,)), 'sw_w1': rn(ks[2], (H, I)), 'sw_w3': rn(ks[3], (H, I)), 'sw_w2': rn(ks[4], (I, H)), 'me_eq_w': rn(ks[5], (H, H)), 'me_eq_b': z((H,)), 'me_wv': rn(ks[6], (H, H)), 'me_bv': z((H,)), 'me_wo': rn(ks[7], (H, H)), 'me_bo': z((H,)), 'me_c1w': rn(ks[8], (H, 2 * H)), 'me_c1b': z((2 * H,)), 'me_c2w': rn(ks[9], (2 * H, H)), 'me_c2b': z((H,)), 'ce_syn_w': rn(ks[10], (H, H)), 'ce_syn_b': z((H,)), 'ce_wv': rn(ks[11], (H, H)), 'ce_bv': z((H,)), 'ce_wo': rn(ks[12], (H, H)), 'ce_bo': z((H,)), 'ce_n1g': o((H,)), 'ce_n1b': z((H,)), 'ce_f1w': rn(ks[13], (H, 2 * H)), 'ce_f1b': z((2 * H,)), 'ce_f2w': rn(ks[14], (2 * H, H)), 'ce_f2b': z((H,)), 'ce_n2g': o((H,)), 'ce_n2b': z((H,)), 'ce_gen_w': rn(ks[15], (H, H)), 'ce_gen_b': z((H,)), 'ml_w1': rn(ks[16], (H, I)), 'ml_b1': z((I,)), 'ml_w2': rn(ks[17], (I, H)), 'ml_b2': z((H,))}
    _L1_ffn_in = _L1_ffn_setup()
    _d = {'L0_attn_x': _L0_attn_in['x'], 'L0_attn_phazor_init_re': _L0_attn_in['phazor_init_re'], 'L0_attn_phazor_init_im': _L0_attn_in['phazor_init_im'], 'L0_attn_phazor_angle': _L0_attn_in['phazor_angle'], 'L0_attn_ln_minus_ln_phazor_abs': _L0_attn_in['ln_minus_ln_phazor_abs'], 'L0_attn_last_conv_re': _L0_attn_in['last_conv_re'], 'L0_attn_last_conv_im': _L0_attn_in['last_conv_im'], 'L0_attn_ln_phazor_scale': _L0_attn_in['ln_phazor_scale'], 'L0_ffn_router': _L0_ffn_in['router'], 'L0_ffn_experts_gate': _L0_ffn_in['experts_gate'], 'L0_ffn_experts_up': _L0_ffn_in['experts_up'], 'L0_ffn_experts_down': _L0_ffn_in['experts_down'], 'L0_ffn_shared_gate': _L0_ffn_in['shared_gate'], 'L0_ffn_shared_up': _L0_ffn_in['shared_up'], 'L0_ffn_shared_down': _L0_ffn_in['shared_down'], 'L1_attn_gamma': _L1_attn_in['gamma'], 'L1_attn_w_q': _L1_attn_in['w_q'], 'L1_attn_w_kv': _L1_attn_in['w_kv'], 'L1_attn_null_kv': _L1_attn_in['null_kv'], 'L1_attn_q_scale': _L1_attn_in['q_scale'], 'L1_attn_k_scale': _L1_attn_in['k_scale'], 'L1_attn_w_out': _L1_attn_in['w_out'], 'L1_ffn_router_w': _L1_ffn_in['router_w'], 'L1_ffn_router_b': _L1_ffn_in['router_b'], 'L1_ffn_load_balancer': _L1_ffn_in['load_balancer'], 'L1_ffn_sw_w1': _L1_ffn_in['sw_w1'], 'L1_ffn_sw_w3': _L1_ffn_in['sw_w3'], 'L1_ffn_sw_w2': _L1_ffn_in['sw_w2'], 'L1_ffn_me_eq_w': _L1_ffn_in['me_eq_w'], 'L1_ffn_me_eq_b': _L1_ffn_in['me_eq_b'], 'L1_ffn_me_wv': _L1_ffn_in['me_wv'], 'L1_ffn_me_bv': _L1_ffn_in['me_bv'], 'L1_ffn_me_wo': _L1_ffn_in['me_wo'], 'L1_ffn_me_bo': _L1_ffn_in['me_bo'], 'L1_ffn_me_c1w': _L1_ffn_in['me_c1w'], 'L1_ffn_me_c1b': _L1_ffn_in['me_c1b'], 'L1_ffn_me_c2w': _L1_ffn_in['me_c2w'], 'L1_ffn_me_c2b': _L1_ffn_in['me_c2b'], 'L1_ffn_ce_syn_w': _L1_ffn_in['ce_syn_w'], 'L1_ffn_ce_syn_b': _L1_ffn_in['ce_syn_b'], 'L1_ffn_ce_wv': _L1_ffn_in['ce_wv'], 'L1_ffn_ce_bv': _L1_ffn_in['ce_bv'], 'L1_ffn_ce_wo': _L1_ffn_in['ce_wo'], 'L1_ffn_ce_bo': _L1_ffn_in['ce_bo'], 'L1_ffn_ce_n1g': _L1_ffn_in['ce_n1g'], 'L1_ffn_ce_n1b': _L1_ffn_in['ce_n1b'], 'L1_ffn_ce_f1w': _L1_ffn_in['ce_f1w'], 'L1_ffn_ce_f1b': _L1_ffn_in['ce_f1b'], 'L1_ffn_ce_f2w': _L1_ffn_in['ce_f2w'], 'L1_ffn_ce_f2b': _L1_ffn_in['ce_f2b'], 'L1_ffn_ce_n2g': _L1_ffn_in['ce_n2g'], 'L1_ffn_ce_n2b': _L1_ffn_in['ce_n2b'], 'L1_ffn_ce_gen_w': _L1_ffn_in['ce_gen_w'], 'L1_ffn_ce_gen_b': _L1_ffn_in['ce_gen_b'], 'L1_ffn_ml_w1': _L1_ffn_in['ml_w1'], 'L1_ffn_ml_b1': _L1_ffn_in['ml_b1'], 'L1_ffn_ml_w2': _L1_ffn_in['ml_w2'], 'L1_ffn_ml_b2': _L1_ffn_in['ml_b2']}
    _x0 = _d['L0_attn_x']
    _d['L0_attn_x'] = jax.random.normal(jax.random.fold_in(jax.random.key(seed), 1), (16, 256, 128), dtype=_x0.dtype)
    del _x0
    return _d

def reference(L0_attn_x, L0_attn_phazor_init_re, L0_attn_phazor_init_im, L0_attn_phazor_angle, L0_attn_ln_minus_ln_phazor_abs, L0_attn_last_conv_re, L0_attn_last_conv_im, L0_attn_ln_phazor_scale, L0_ffn_router, L0_ffn_experts_gate, L0_ffn_experts_up, L0_ffn_experts_down, L0_ffn_shared_gate, L0_ffn_shared_up, L0_ffn_shared_down, L1_attn_gamma, L1_attn_w_q, L1_attn_w_kv, L1_attn_null_kv, L1_attn_q_scale, L1_attn_k_scale, L1_attn_w_out, L1_ffn_router_w, L1_ffn_router_b, L1_ffn_load_balancer, L1_ffn_sw_w1, L1_ffn_sw_w3, L1_ffn_sw_w2, L1_ffn_me_eq_w, L1_ffn_me_eq_b, L1_ffn_me_wv, L1_ffn_me_bv, L1_ffn_me_wo, L1_ffn_me_bo, L1_ffn_me_c1w, L1_ffn_me_c1b, L1_ffn_me_c2w, L1_ffn_me_c2b, L1_ffn_ce_syn_w, L1_ffn_ce_syn_b, L1_ffn_ce_wv, L1_ffn_ce_bv, L1_ffn_ce_wo, L1_ffn_ce_bo, L1_ffn_ce_n1g, L1_ffn_ce_n1b, L1_ffn_ce_f1w, L1_ffn_ce_f1b, L1_ffn_ce_f2w, L1_ffn_ce_f2b, L1_ffn_ce_n2g, L1_ffn_ce_n2b, L1_ffn_ce_gen_w, L1_ffn_ce_gen_b, L1_ffn_ml_w1, L1_ffn_ml_b1, L1_ffn_ml_w2, L1_ffn_ml_b2):

    def _L0_attn_ref(x, phazor_init_re, phazor_init_im, phazor_angle, ln_minus_ln_phazor_abs, last_conv_re, last_conv_im, ln_phazor_scale):
        import jax, jax.numpy as jnp
        import numpy as np
        B, L, D = (4, 512, 128)
        PHAZOR_SCALE_START = 32.0
        PHAZOR_SCALE_END = 2048.0
        b, length, d = x.shape
        dtype = x.dtype
        xc = x.astype(jnp.complex64)
        decay = jnp.exp(ln_minus_ln_phazor_abs)
        phazor = jnp.exp((phazor_angle * 1j - decay) * ln_phazor_scale)
        t = jnp.arange(length, dtype=jnp.float32)[:, None]
        phazor_progression = phazor[None, :] ** t
        phazor_init = phazor_init_re + 1j * phazor_init_im
        filt = phazor_progression * phazor_init[None, :]
        filter_fft = jnp.fft.fft(filt, n=2 * length, axis=0)
        x_fft = jnp.fft.fft(xc, n=2 * length, axis=1)
        conv_filter_x = jnp.fft.ifft(filter_fft[None] * x_fft, axis=1)[:, :length]
        last_conv = (last_conv_re + 1j * last_conv_im)[None, None, :]
        conv_with_past = conv_filter_x + last_conv * phazor_progression[None] * phazor[None, None, :]
        gate = 1.0 - jnp.exp(-decay * ln_phazor_scale)
        y = conv_with_past * gate
        return y.real.astype(dtype)

    def _L0_ffn_ref(x, router, experts_gate, experts_up, experts_down, shared_gate, shared_up, shared_down):
        import jax, jax.numpy as jnp
        import numpy as np
        TOP_K = 2
        NUM_EXPERTS = 8
        b, s, h = x.shape
        E = router.shape[1]
        shared_act = jax.nn.silu(jnp.einsum('bsh,hd->bsd', x, shared_gate))
        shared_up_out = jnp.einsum('bsh,hd->bsd', x, shared_up)
        shared_out = jnp.einsum('bsd,dh->bsh', shared_act * shared_up_out, shared_down)
        router_probs = jax.nn.softmax(jnp.einsum('bsh,he->bse', x, router), axis=-1)
        topk_probs, topk_idx = jax.lax.top_k(router_probs, TOP_K)
        coef = jnp.sum(jax.nn.one_hot(topk_idx, E, dtype=x.dtype) * topk_probs[..., None], axis=2)
        coef = coef.reshape(b * s, E)
        x_flat = x.reshape(b * s, h)
        gate = jnp.einsum('th,ehd->etd', x_flat, experts_gate)
        up = jnp.einsum('th,ehd->etd', x_flat, experts_up)
        expert_out = jnp.einsum('etd,edh->eth', jax.nn.silu(gate) * up, experts_down)
        routed = jnp.einsum('eth,te->th', expert_out, coef)
        return routed.reshape(b, s, h) + shared_out

    def _L1_attn_ref(x, gamma, w_q, w_kv, null_kv, q_scale, k_scale, w_out):
        import math
        import jax, jax.numpy as jnp
        import numpy as np
        HEADS = 16
        DIM_HEAD = 64
        NUM_NULL_KV = 2
        ATTN_SCALE = 8.0
        LN_EPS = 1e-05

        def _alibi_slopes(heads):
            start = 2.0 ** (-2.0 ** (-(math.log2(heads) - 3.0)))
            return np.array([start * start ** i for i in range(heads)], dtype=np.float32)

        def _l2norm(t):
            return t / jnp.maximum(jnp.linalg.norm(t, axis=-1, keepdims=True), 1e-12)
        b, n, dim = x.shape
        mu = jnp.mean(x, axis=-1, keepdims=True)
        var = jnp.mean(jnp.square(x - mu), axis=-1, keepdims=True)
        xn = (x - mu) * jax.lax.rsqrt(var + LN_EPS) * gamma
        q = (xn @ w_q).reshape(b, n, HEADS, DIM_HEAD).transpose(0, 2, 1, 3)
        kv = xn @ w_kv
        k, v = jnp.split(kv, 2, axis=-1)
        k = k.reshape(b, n, HEADS, DIM_HEAD).transpose(0, 2, 1, 3)
        v = v.reshape(b, n, HEADS, DIM_HEAD).transpose(0, 2, 1, 3)
        nkv = null_kv.reshape(HEADS, NUM_NULL_KV, 2, DIM_HEAD)
        nk = jnp.broadcast_to(nkv[:, :, 0][None], (b, HEADS, NUM_NULL_KV, DIM_HEAD))
        nv = jnp.broadcast_to(nkv[:, :, 1][None], (b, HEADS, NUM_NULL_KV, DIM_HEAD))
        k = jnp.concatenate([nk, k], axis=2)
        v = jnp.concatenate([nv, v], axis=2)
        q = _l2norm(q) * q_scale
        k = _l2norm(k) * k_scale
        sim = jnp.einsum('bhid,bhjd->bhij', q, k) * ATTN_SCALE
        j = n + NUM_NULL_KV
        rows = jnp.arange(n)
        cols = jnp.arange(j)
        dist = -jnp.abs(cols[None, :] - (rows[:, None] + NUM_NULL_KV)).astype(sim.dtype)
        slopes = jnp.asarray(_alibi_slopes(HEADS))
        sim = sim + dist[None, None] * slopes[None, :, None, None]
        causal_mask = cols[None, :] > rows[:, None] + NUM_NULL_KV
        neg = -jnp.finfo(sim.dtype).max
        sim = jnp.where(causal_mask[None, None], neg, sim)
        attn = jax.nn.softmax(sim, axis=-1)
        out = jnp.einsum('bhij,bhjd->bhid', attn, v)
        out = out.transpose(0, 2, 1, 3).reshape(b, n, HEADS * DIM_HEAD)
        return out @ w_out

    def _L1_ffn_ref(x, router_w, router_b, load_balancer, sw_w1, sw_w3, sw_w2, me_eq_w, me_eq_b, me_wv, me_bv, me_wo, me_bo, me_c1w, me_c1b, me_c2w, me_c2b, ce_syn_w, ce_syn_b, ce_wv, ce_bv, ce_wo, ce_bo, ce_n1g, ce_n1b, ce_f1w, ce_f1b, ce_f2w, ce_f2b, ce_n2g, ce_n2b, ce_gen_w, ce_gen_b, ml_w1, ml_b1, ml_w2, ml_b2):
        import jax, jax.numpy as jnp
        import numpy as np
        B, S, H, I, E, K = (4, 256, 128, 512, 4, 2)

        def _layer_norm(h, g, b, eps=1e-05):
            mu = h.mean(-1, keepdims=True)
            var = ((h - mu) ** 2).mean(-1, keepdims=True)
            return (h - mu) * jax.lax.rsqrt(var + eps) * g + b
        logits = jnp.einsum('bsh,he->bse', x, router_w) + router_b + load_balancer
        rw, sel = jax.lax.top_k(logits, K)
        rw = jax.nn.softmax(rw, axis=-1)
        e0 = jax.nn.silu(x @ sw_w1) * (x @ sw_w3) @ sw_w2
        eq = x @ me_eq_w + me_eq_b
        sym = (eq @ me_wv + me_bv) @ me_wo + me_bo
        e1 = jax.nn.gelu(sym @ me_c1w + me_c1b, approximate=False) @ me_c2w + me_c2b
        syn = x @ ce_syn_w + ce_syn_b
        attn = (syn @ ce_wv + ce_bv) @ ce_wo + ce_bo
        h2 = _layer_norm(syn + attn, ce_n1g, ce_n1b)
        ff = jax.nn.relu(h2 @ ce_f1w + ce_f1b) @ ce_f2w + ce_f2b
        h2 = _layer_norm(h2 + ff, ce_n2g, ce_n2b)
        e2 = h2 @ ce_gen_w + ce_gen_b
        e3 = jax.nn.gelu(x @ ml_w1 + ml_b1, approximate=False) @ ml_w2 + ml_b2
        stack = jnp.stack([e0, e1, e2, e3], axis=2)
        gathered = jnp.take_along_axis(stack, sel[..., None], axis=2)
        return (rw[..., None] * gathered).sum(axis=2)
    x = L0_attn_x
    x = x + _layernorm(_L0_attn_ref(_layernorm(x, axis=-1), L0_attn_phazor_init_re, L0_attn_phazor_init_im, L0_attn_phazor_angle, L0_attn_ln_minus_ln_phazor_abs, L0_attn_last_conv_re, L0_attn_last_conv_im, L0_attn_ln_phazor_scale), axis=-1)
    x = x + _layernorm(_L0_ffn_ref(_layernorm(x, axis=-1), L0_ffn_router, L0_ffn_experts_gate, L0_ffn_experts_up, L0_ffn_experts_down, L0_ffn_shared_gate, L0_ffn_shared_up, L0_ffn_shared_down), axis=-1)
    x = x + _layernorm(_L1_attn_ref(_layernorm(x, axis=-1), L1_attn_gamma, L1_attn_w_q, L1_attn_w_kv, L1_attn_null_kv, L1_attn_q_scale, L1_attn_k_scale, L1_attn_w_out), axis=-1)
    x = x + _layernorm(_L1_ffn_ref(_layernorm(x, axis=-1), L1_ffn_router_w, L1_ffn_router_b, L1_ffn_load_balancer, L1_ffn_sw_w1, L1_ffn_sw_w3, L1_ffn_sw_w2, L1_ffn_me_eq_w, L1_ffn_me_eq_b, L1_ffn_me_wv, L1_ffn_me_bv, L1_ffn_me_wo, L1_ffn_me_bo, L1_ffn_me_c1w, L1_ffn_me_c1b, L1_ffn_me_c2w, L1_ffn_me_c2b, L1_ffn_ce_syn_w, L1_ffn_ce_syn_b, L1_ffn_ce_wv, L1_ffn_ce_bv, L1_ffn_ce_wo, L1_ffn_ce_bo, L1_ffn_ce_n1g, L1_ffn_ce_n1b, L1_ffn_ce_f1w, L1_ffn_ce_f1b, L1_ffn_ce_f2w, L1_ffn_ce_f2b, L1_ffn_ce_n2g, L1_ffn_ce_n2b, L1_ffn_ce_gen_w, L1_ffn_ce_gen_b, L1_ffn_ml_w1, L1_ffn_ml_b1, L1_ffn_ml_w2, L1_ffn_ml_b2), axis=-1)
    return x

_drawn_inputs = setup_inputs


def setup_inputs(seed=0):
    import zlib

    import numpy as np

    out = dict(_drawn_inputs(seed))
    spreads = {'L1_attn_gamma': (1.0, 0.2),
     'L1_attn_q_scale': (1.0, 0.2),
     'L1_attn_k_scale': (1.0, 0.2),
     'L1_ffn_router_b': (0.0, 0.1),
     'L1_ffn_load_balancer': (1.0, 0.2),
     'L1_ffn_me_eq_b': (0.0, 0.8),
     'L1_ffn_me_bv': (0.0, 2.0),
     'L1_ffn_me_bo': (0.0, 2.0),
     'L1_ffn_me_c1b': (0.0, 2.0),
     'L1_ffn_me_c2b': (0.0, 0.8),
     'L1_ffn_ce_syn_b': (0.0, 0.1),
     'L1_ffn_ce_bv': (0.0, 0.308),
     'L1_ffn_ce_bo': (0.0, 0.1),
     'L1_ffn_ce_n1g': (1.0, 0.2),
     'L1_ffn_ce_n1b': (0.0, 0.1),
     'L1_ffn_ce_f1b': (0.0, 0.8),
     'L1_ffn_ce_f2b': (0.0, 0.1),
     'L1_ffn_ce_n2g': (1.0, 0.2),
     'L1_ffn_ce_n2b': (0.0, 0.1),
     'L1_ffn_ce_gen_b': (0.0, 0.1),
     'L1_ffn_ml_b1': (0.0, 0.1),
     'L1_ffn_ml_b2': (0.0, 0.1)}
    factors = {'L1_ffn_sw_w1': 5.23,
     'L1_ffn_sw_w3': 5.212,
     'L1_ffn_sw_w2': 5.193,
     'L1_ffn_me_eq_w': 8.0,
     'L1_ffn_me_wv': 8.0,
     'L1_ffn_me_wo': 8.0,
     'L1_ffn_me_c1w': 8.0,
     'L1_ffn_me_c2w': 8.0,
     'L1_ffn_ce_wv': 3.187,
     'L1_ffn_ce_f1w': 3.378}
    for name, (base, spread) in spreads.items():
        noise = np.random.default_rng([zlib.crc32(name.encode()), seed]).standard_normal(out[name].shape)
        drawn = base * np.exp(spread * noise) if base else spread * noise
        out[name] = jnp.asarray(drawn.astype(out[name].dtype))
    for name, factor in factors.items():
        out[name] = (out[name] * factor).astype(out[name].dtype)
    return out
```

```python
from contextlib import ExitStack

import numpy as np
from concourse import mybir

F32 = mybir.dt.float32
I32 = mybir.dt.int32
U32 = mybir.dt.uint32
ALU = mybir.AluOpType
ACT = mybir.ActivationFunctionType
AX_X = mybir.AxisListType.X

P = 128
EPS = 1e-5
TWO_PI = 6.283185307179586
ROUND = 12582912.0


class Signal:

    def __init__(self, sem, per):
        self.sem, self.per = sem, per

    def at(self, g, n=None):
        return g * self.per + (self.per if n is None else n)


class Norm:

    def __init__(self, sb, signal, name, more=0, twice=False):
        self.six = sb(name + "_six", [P, 4, 6])
        self.mv = sb(name + "_mv", [P, 4, 2])
        self.var = sb(name + "_var", [P, 4])
        self.rstd = sb(name + "_rstd", [P, 4])
        self.steps = signal(name + "_steps", 13 + more)
        self.rooted = signal(name + "_rooted", 1)
        self.scale, self.add = (1.0 + EPS, EPS * EPS) if twice else (1.0, EPS)


def program(nc, a, out, store_what="x4"):
    x = a["L0_attn_x"]
    B, L, D = x.shape
    SEQ = 2
    G = B // SEQ
    T = SEQ * L // P
    N = T * P
    H, DH, NULLS = 16, 64, 2
    E0 = a["L0_ffn_router"].shape[1]
    HID0 = a["L0_ffn_experts_gate"].shape[2] * E0
    J0 = HID0 // P
    I1 = a["L1_ffn_sw_w1"].shape[1]
    J1 = I1 // P
    E1 = a["L1_ffn_router_w"].shape[1]
    assert D == P and L == 2 * P and T == 4 and N == 512 and E0 == 8 and G >= 3

    start = 2.0 ** (-2.0 ** (-1.0))
    SLOPES = [start * start ** i for i in range(H)]
    MID = P // 2 - 1

    with ExitStack() as ctx:
        def sb(name, shape, dt=F32):
            return ctx.enter_context(nc.sbuf_tensor(name, shape, dt))

        def sem(name):
            return ctx.enter_context(nc.semaphore(name))

        def signal(name, per):
            return Signal(sem(name), per)

        bank = [ctx.enter_context(nc.psum_tensor(f"bank{i}", [P, 512], F32)) for i in range(8)]

        ident = sb("ident", [P, P])
        causal = sb("causal", [P, P])
        expert_no = sb("expert_no", [P, 4, 8])
        minus_half = sb("minus_half", [P, 16])
        sel = sb("sel", [E0, HID0])
        part_no = sb("part_no", [P, 1])
        zero_col = sb("zero_col", [P, 1])
        cos_t = sb("cos_t", [P, L + 1])
        sin_t = sb("sin_t", [P, L + 1])
        conv_a = sb("conv_a", [P, L])
        conv_b = sb("conv_b", [P, L])
        conv_c = sb("conv_c", [P, L])
        decay_row = sb("decay_row", [P, N])
        vec = sb("vec", [P, 40])
        slope = sb("slope", [P, H])
        bias_diag = sb("bias_diag", [P, H])
        bias_off = sb("bias_off", [P, H])
        bias_null = sb("bias_null", [P, T, H, NULLS])
        qk_scale = sb("qk_scale", [P, 1])
        w0_router = sb("w0_router", [P, E0])
        w0_gate = sb("w0_gate", [P, HID0 + P])
        w0_up = sb("w0_up", [P, HID0 + P])
        w0_down = sb("w0_down", [P, J0 + 1, P])
        w_q = sb("w_q", [P, H * DH])
        w_kv = sb("w_kv", [P, 2 * H * DH])
        w_out = sb("w_out", [P, H * DH // P, P])
        w_nk = sb("w_nk", [P, H * NULLS])
        w_nv = sb("w_nv", [H * NULLS, P])
        w1_router = sb("w1_router", [P, 8])
        b1_router = sb("b1_router", [P, 8])
        w_sw1 = sb("w_sw1", [P, I1])
        w_sw3 = sb("w_sw3", [P, I1])
        w_sw2 = sb("w_sw2", [P, J1, P])
        w_me = sb("w_me", [P, 2 * P])
        w_c2 = sb("w_c2", [P, 2, P])
        w_ce = sb("w_ce", [P, P])
        w_f1 = sb("w_f1", [P, 2 * P])
        w_f2 = sb("w_f2", [P, 2, P])
        w_gen = sb("w_gen", [P, P])
        w_ml1 = sb("w_ml1", [P, I1])
        w_ml2 = sb("w_ml2", [P, J1, P])
        b_me = sb("b_me", [P, 2])
        b_f1 = sb("b_f1", [P, 2])
        b_ml = sb("b_ml", [P, J1])
        row_ce = sb("row_ce", [P, P])
        row_g1 = sb("row_g1", [P, P])
        row_res = sb("row_res", [P, P])
        row_out = sb("row_out", [P, E1, P])

        xin = sb("xin", [P, T, D])
        xn = sb("xn", [P, T, D])
        x1 = sb("x1", [P, T, D])
        x2n = sb("x2n", [P, T, D])
        x2 = sb("x2", [P, T, D])
        x3 = sb("x3", [P, T, D])
        x4 = sb("x4", [P, T, D])
        x4m = sb("x4m", [P, T, D])
        xa = sb("xa", [P, T, D])
        xlT = sb("xlT", [P, N])
        xaT = sb("xaT", [P, N])
        xmT = sb("xmT", [P, N])
        conv = sb("conv", [P, 4, N])
        tanh0 = sb("tanh0", [P, N])
        hid0 = sb("hid0", [P, J0 + 1, N])
        logit0 = sb("logit0", [P, T, 8])
        top0 = sb("top0", [P, T, 8])
        idx0 = sb("idx0", [P, T, 8], U32)
        idf0 = sb("idf0", [P, T, 2])
        exp0 = sb("exp0", [P, T, 8])
        sum0 = sb("sum0", [P, T])
        prob0 = sb("prob0", [P, T, 2])
        pick0 = sb("pick0", [P, 2, T, 8])
        coef0T = sb("coef0T", [E0, N])
        square = sb("square", [P, 2, 512])
        sumsq = sb("sumsq", [P, 2, 16])
        rnorm = sb("rnorm", [P, 2, T, 16])
        unit = sb("unit", [P, 4, 512])
        qT = sb("qT", [P, 8, N])
        kT = sb("kT", [P, 8, N])
        val = sb("val", [P, T, H, DH + 1])
        null_s = sb("null_s", [P, T, H, NULLS])
        null_p = sb("null_p", [P, T, H, NULLS])
        null_sum = sb("null_sum", [P, T, H])
        null_pT = sb("null_pT", [H * NULLS, N])
        p_diag = sb("p_diag", [P, 2, N])
        p_off = sb("p_off", [P, 2, 2 * P])
        denom = sb("denom", [P, T])
        recip = sb("recip", [P, T, H])
        mixed = sb("mixed", [P, T, H * DH])
        logit1 = sb("logit1", [P, T, 8])
        top1 = sb("top1", [P, T, 8])
        idx1 = sb("idx1", [P, T, 8], U32)
        idf1 = sb("idf1", [P, T, 2])
        gap1 = sb("gap1", [P, T])
        wt1 = sb("wt1", [P, T, 2])
        pick1 = sb("pick1", [P, 2, T, 8])
        mixed_flat = mixed[:].rearrange("p t c -> p (t c)").rearrange("p (j n) -> p j n", n=N)
        hid_sw = [mixed_flat[:, j, :] for j in range(4)]
        hid_me = [mixed_flat[:, 4 + j, :] for j in range(2)]
        hid_relu = [mixed_flat[:, 6 + j, :] for j in range(2)]
        hid_ml = [hid0[:, j, :] for j in range(4)]
        tanh1 = hid0[:, 4, :]
        ce_rows = conv[:, 0, :].rearrange("p (t d) -> p t d", t=T)
        ce_T = conv[:, 1, :]
        ce_res = conv[:, 2, :].rearrange("p (t d) -> p t d", t=T)
        mix_e = conv[:, 3, :].rearrange("p (e d) -> p e d", e=E1)
        outT = qT

        vlist = ["angle", "lnabs", "scale", "init_re", "init_im", "last_re", "last_im", "decay", "z",
                 "nz", "theta", "r", "gate", "gamma", "qs", "ks", "eq_b", "me_bv", "me_bo", "syn_b",
                 "ce_bv", "n1b", "n2b", "n1g", "n2g"]
        col = {n: vec[:, i:i + 1] for i, n in enumerate(vlist)}
        c1b = vec[:, 26:28]
        f1b = vec[:, 28:30]

        nk_rows = mixed[0:32, 0, 0:64]
        nv_rows = mixed[0:32, 0, 64:128]
        qs_row = mixed[0:32, 0, 128:192]
        ks_row = mixed[0:32, 0, 192:256]
        nk_sq = mixed[0:32, 0, 256:320]
        nk_z = mixed[0:32, 0, 320:448]
        nv_z = mixed[0:32, 0, 448:576]
        par_i = sb("par_i", [32, 2], I32)
        par = mixed[0:32, 0, 576:578]
        nk_ss = mixed[0:32, 0, 578:580]
        nk_zT = mixed[:, 0, 640:672]
        nv_zT = mixed[:, 0, 672:704]
        nv_pad = mixed[:, 1, 0:256].rearrange("p (c r) -> p c r", c=8)
        me_raw = [mixed[:, 2, 128 * i:128 * i + 128] for i in range(3)]
        me_c1 = mixed[:, 2, 384:640]
        me_p1 = mixed[:, 2, 640:896]
        me_p2 = mixed[:, 3, 0:256]
        ce_raw = [mixed[:, 3, 256 + 128 * i:384 + 128 * i] for i in range(3)]
        ce_v2 = mixed[:, 3, 640:768]
        time = kT[:, 0, 0:L + 1]
        phase = kT[:, 1, 0:L + 1]
        turns = kT[:, 2, 0:L + 1]
        frac = kT[:, 3, 0:L + 1]
        rpow = kT[:, 4, 0:L + 1]
        part_a = kT[:, 5, 0:L + 1]
        part_b = kT[:, 6, 0:L + 1]
        wT = [kT[:, 7, 128 * i:128 * i + 128] for i in range(4)] + [qT[:, 7, 128 * i:128 * i + 128] for i in range(3)]
        wqT = qT[:, 0:2, :].rearrange("p a (c n) -> p (a c) n", n=P)
        colb = [qT[:, 2, 128 * i:128 * i + 128] for i in range(3)]
        row_tmp = [qT[:, 3, 128 * i:128 * i + 128] for i in range(4)]
        lb_row = qT[:, 4, 0:8]
        zraw = sb("zraw", [P, 2])

        loaded0 = sem("loaded0")
        loaded1 = sem("loaded1")
        loaded2 = sem("loaded2")
        made = sem("made")
        pool_made = sem("pool_made")
        act_made = sem("act_made")
        pe_made = sem("pe_made")
        all_set = sem("all_set")
        dve_passed = sem("dve_passed")
        pool_passed = sem("pool_passed")

        x_loaded = signal("x_loaded", 16)
        stored = signal("stored", 16)
        n_x = Norm(sb, signal, "n_x")
        n_y = Norm(sb, signal, "n_y", more=1)
        n_l = Norm(sb, signal, "n_l")
        n_d = Norm(sb, signal, "n_d", more=1)
        n_a = Norm(sb, signal, "n_a", twice=True)
        n_o = Norm(sb, signal, "n_o", more=1)
        n_m = Norm(sb, signal, "n_m")
        n_c = Norm(sb, signal, "n_c")
        n_c2 = Norm(sb, signal, "n_c2")
        n_f = Norm(sb, signal, "n_f", more=1)
        l_turned = signal("l_turned", 3)
        l_conv = signal("l_conv", 6)
        l_gain = signal("l_gain", 2)
        l_cols = signal("l_cols", 2)
        l_routed = signal("l_routed", 2)
        l_pick = signal("l_pick", 10 + 2 * T)
        l_coefd = signal("l_coefd", 1)
        l_exp = signal("l_exp", 1)
        l_gu = signal("l_gu", J0 + 1)
        l_tanh = signal("l_tanh", J0 + 1)
        l_hid = signal("l_hid", 3 * J0 + 2)
        l_down = signal("l_down", 1)
        a_kept = signal("a_kept", 1)
        a_turned = signal("a_turned", 1)
        a_cols = signal("a_cols", 1)
        a_nulls = signal("a_nulls", 1)
        a_nullc = signal("a_nullc", 4)
        a_nexp = signal("a_nexp", 1)
        a_proj = signal("a_proj", 4 * T)
        a_sq = signal("a_sq", 4 * T)
        a_ss = signal("a_ss", 6 * T)
        a_root = signal("a_root", 2 * T)
        a_unit = signal("a_unit", 4 * T)
        a_turn = signal("a_turn", 4 * T)
        a_flat = signal("a_flat", 4 * T)
        a_v = signal("a_v", 2 * T)
        a_vals = signal("a_vals", 2 * T)
        a_s = signal("a_s", 2 * H)
        a_exp = signal("a_exp", 2 * H)
        a_mask = signal("a_mask", H)
        a_pv = signal("a_pv", H)
        a_mix = signal("a_mix", 3 * H)
        a_pn = signal("a_pn", 1)
        a_oT = signal("a_oT", 9)
        a_oc = signal("a_oc", 9)
        a_out = signal("a_out", 1)
        f_turned = signal("f_turned", 1)
        f_cols = signal("f_cols", 1)
        f_routed = signal("f_routed", 1)
        f_pick = signal("f_pick", 9 + 2 * T)
        f_coefd = signal("f_coefd", 1)
        f_gap = signal("f_gap", 1)
        f_gu = signal("f_gu", J1)
        f_tanh = signal("f_tanh", J1)
        f_hid = signal("f_hid", 2 * J1)
        f_me = signal("f_me", 2)
        f_meg = signal("f_meg", 2)
        f_ml = signal("f_ml", J1)
        f_mlg = signal("f_mlg", J1)
        f_ce = signal("f_ce", 3)
        f_ced = signal("f_ced", 2)
        f_res = signal("f_res", 2)
        f_cec = signal("f_cec", 2)
        f_r = signal("f_r", 2)
        f_relu = signal("f_relu", 2)
        f_gT = signal("f_gT", 1)
        f_e = signal("f_e", T)
        f_eb = signal("f_eb", 2 * T)
        f_ew = signal("f_ew", T)

        def rows3(ap):
            return ap.rearrange("p (t d) -> p t d", t=T)

        LOADS2 = 50
        POOL_MADE = 8 + H + 5 + 4
        ACT_MADE = 17
        MADE_FRAC = 4 + 10
        MADE_NKSS = MADE_FRAC + 18 + T * NULLS + 1 + 9
        MADE_RAW = MADE_NKSS + 3 + 2 + 4 + 3
        MADE_PAD = MADE_RAW + 8
        MADE_V2 = MADE_PAD + 1

        block = ctx.enter_context(nc.Block())

        def order(l, m, f):
            S = []

            def put(*steps):
                for s in steps:
                    st = s[0][0]
                    if {"l": l, "a": m, "f": f}[st]:
                        S.append(s)

            put(("a_stats",), ("f_stats",), ("a_apply",), ("f_apply",), ("a_null",))
            put(("a_proj", 0), ("f_route",), ("f_ce",), ("f_sw", 0), ("a_turn", 0), ("f_sw", 1), ("a_value", 0))
            put(("a_proj", 1), ("f_pick",), ("f_sw", 2), ("f_ce_apply",), ("a_turn", 1), ("f_sw", 3), ("a_value", 1))
            put(("a_proj", 2), ("f_relu", 0), ("f_me", 0), ("f_relu", 1), ("a_turn", 2), ("f_me", 1), ("f_ce2",), ("f_ml", 0), ("a_value", 2))
            put(("a_proj", 3), ("f_ml", 1), ("f_ce2_apply",), ("a_turn", 3), ("f_ml", 2), ("f_ml", 3), ("a_value", 3))
            put(("f_out", 0), ("f_out", 1), ("a_nexp",), ("f_out", 2), ("f_out", 3))
            put(("a_scores", 0), ("f_end_stats",))
            ls = {0: [("l_stats",)], 1: [("l_apply",)], 2: [("l_scan",)], 3: [("l_back",)],
                  4: [("l_res",)], 5: [("l_norm",)], 6: [("l_route",)], 7: [("l_coef",)], 8: [("l_chunk", 0)],
                  9: [("l_chunk", 1)], 10: [("l_chunk", 2)], 11: [("l_chunk", 3)], 12: [("l_chunk", 4)],
                  13: [("l_down",)], 14: [("l_end",)]}
            for h in range(H):
                if h + 1 < H:
                    put(("a_scores", h + 1))
                if h == 0:
                    put(("f_end",))
                put(("a_mix", h))
                put(*ls.get(h, []))
            put(("a_oT",), ("a_out",), ("a_end",))
            return S

        def play(steps, S, l, m, f):
            group = {"l": l, "a": m, "f": f}
            for s in S:
                if s[0] in steps:
                    steps[s[0]](group[s[0][0]], *s[1:])

        def plan(eng, steps):
            play(steps, order(1, 0, 0), 0, None, None)
            play(steps, order(1, 1, 0), 1, 0, None)
            with eng.Fori(1, G - 1) as i:
                play(steps, order(1, 1, 1), i + 1, i, i - 1)
            play(steps, order(0, 1, 1), None, G - 1, G - 2)
            play(steps, order(0, 0, 1), None, None, G - 1)

        def known(g):
            return isinstance(g, int)

        def first(g):
            return known(g) and g == 0

        xv = x.rearrange("(g s) (b p) d -> g p (s b) d", s=SEQ, p=P)
        ov = out.rearrange("(g s) (b p) d -> g p (s b) d", s=SEQ, p=P)

        @block.sync
        def _(sp):
            def load_x(g):
                if not first(g):
                    sp.wait_ge(n_y.steps.sem, n_y.steps.at(g - 1))
                sp.dma_start(xin[:], xv[g]).then_inc(x_loaded.sem, 16)

            def store(g):
                sp.wait_ge(n_f.steps.sem, n_f.steps.at(g))
                sp.dma_start(ov[g], {"x1": x1, "x2": x2n, "x3": x3, "x4": x4}[store_what][:]).then_inc(stored.sem, 16)

            column = lambda v: v.rearrange("(p a) -> p a", a=1)
            columns = lambda v: v.rearrange("(c p) -> p c", p=P)
            row = lambda v, n=P: v.partition_broadcast(n)

            sp.sem_inc(stored.sem, stored.per)
            load_x(0)
            for name, v in (("lnabs", "L0_attn_ln_minus_ln_phazor_abs"), ("angle", "L0_attn_phazor_angle"),
                            ("scale", "L0_attn_ln_phazor_scale"), ("init_re", "L0_attn_phazor_init_re"),
                            ("init_im", "L0_attn_phazor_init_im"), ("last_re", "L0_attn_last_conv_re"),
                            ("last_im", "L0_attn_last_conv_im")):
                sp.dma_start(col[name], column(a[v])).then_inc(loaded0, 16)
            for dst, src in (
                (w0_router[:], a["L0_ffn_router"]),
                (w0_gate[:, 0:HID0].rearrange("p (e d) -> p e d", e=E0), a["L0_ffn_experts_gate"].rearrange("e h d -> h e d")),
                (w0_up[:, 0:HID0].rearrange("p (e d) -> p e d", e=E0), a["L0_ffn_experts_up"].rearrange("e h d -> h e d")),
                (w0_gate[:, HID0:], a["L0_ffn_shared_gate"]),
                (w0_up[:, HID0:], a["L0_ffn_shared_up"]),
                (w0_down[:, 0:J0, :], a["L0_ffn_experts_down"].rearrange("e d h -> (e d) h").rearrange("(j p) h -> p j h", p=P)),
                (w0_down[:, J0, :], a["L0_ffn_shared_down"]),
            ):
                sp.dma_start(dst, src).then_inc(loaded1, 16)
            nkv = a["L1_attn_null_kv"].rearrange("h (n two) d -> (h n) two d", two=2)
            loads = [
                (w_q[:], a["L1_attn_w_q"]), (w_kv[:], a["L1_attn_w_kv"]),
                (w_out[:], a["L1_attn_w_out"].rearrange("(c p) d -> p c d", p=P)),
                (col["gamma"], column(a["L1_attn_gamma"])),
                (vec[0:64, 14:15], column(a["L1_attn_q_scale"])), (vec[64:128, 14:15], column(a["L1_attn_q_scale"])),
                (vec[0:64, 15:16], column(a["L1_attn_k_scale"])), (vec[64:128, 15:16], column(a["L1_attn_k_scale"])),
                (qs_row, row(a["L1_attn_q_scale"], 32)), (ks_row, row(a["L1_attn_k_scale"], 32)),
                (nk_rows, nkv[:, 0, :]), (nv_rows, nkv[:, 1, :]),
                (w1_router[:, 0:E1], a["L1_ffn_router_w"]),
                (b1_router[:, 0:E1], row(a["L1_ffn_router_b"])), (lb_row[:, 0:E1], row(a["L1_ffn_load_balancer"])),
                (w_sw1[:], a["L1_ffn_sw_w1"]), (w_sw3[:], a["L1_ffn_sw_w3"]),
                (w_sw2[:], a["L1_ffn_sw_w2"].rearrange("(c p) d -> p c d", p=P)),
                (me_raw[0], a["L1_ffn_me_eq_w"]), (me_raw[1], a["L1_ffn_me_wv"]), (me_raw[2], a["L1_ffn_me_wo"]),
                (me_c1, a["L1_ffn_me_c1w"]), (w_c2[:], a["L1_ffn_me_c2w"].rearrange("(c p) d -> p c d", p=P)),
                (col["eq_b"], column(a["L1_ffn_me_eq_b"])), (col["me_bv"], column(a["L1_ffn_me_bv"])),
                (col["me_bo"], column(a["L1_ffn_me_bo"])), (c1b, columns(a["L1_ffn_me_c1b"])),
                (ce_raw[0], a["L1_ffn_ce_syn_w"]), (ce_raw[1], a["L1_ffn_ce_wv"]), (ce_raw[2], a["L1_ffn_ce_wo"]),
                (col["syn_b"], column(a["L1_ffn_ce_syn_b"])), (col["ce_bv"], column(a["L1_ffn_ce_bv"])),
                (row_tmp[0], row(a["L1_ffn_ce_bo"])), (row_tmp[1], row(a["L1_ffn_ce_f2b"])),
                (row_tmp[2], row(a["L1_ffn_ce_gen_b"])), (row_tmp[3], row(a["L1_ffn_ce_n1b"])),
                (row_g1[:], row(a["L1_ffn_ce_n1g"])),
                (col["n1g"], column(a["L1_ffn_ce_n1g"])), (col["n1b"], column(a["L1_ffn_ce_n1b"])),
                (col["n2g"], column(a["L1_ffn_ce_n2g"])), (col["n2b"], column(a["L1_ffn_ce_n2b"])),
                (w_f1[:], a["L1_ffn_ce_f1w"]), (w_f2[:], a["L1_ffn_ce_f2w"].rearrange("(c p) d -> p c d", p=P)),
                (f1b, columns(a["L1_ffn_ce_f1b"])), (w_gen[:], a["L1_ffn_ce_gen_w"]),
                (w_ml1[:], a["L1_ffn_ml_w1"]), (w_ml2[:], a["L1_ffn_ml_w2"].rearrange("(c p) d -> p c d", p=P)),
                (b_ml[:], columns(a["L1_ffn_ml_b1"])),
                (row_out[:, 1, :], row(a["L1_ffn_me_c2b"])), (row_out[:, 3, :], row(a["L1_ffn_ml_b2"])),
            ]
            for dst, src in loads:
                sp.dma_start(dst, src, allow_slow_non_contiguous=True).then_inc(loaded2, 16)
            assert len(loads) == LOADS2
            load_x(1)
            with sp.Fori(1, G - 1) as i:
                load_x(i + 1)
                store(i - 1)
            store(G - 2)
            store(G - 1)
            sp.wait_ge(stored.sem, stored.at(G))

        @block.gpsimd
        def _(pool):
            n = [0]

            def made_by(i):
                n[0] += 1
                i.then_inc(pool_made, 1)

            made_by(pool.memset(ident[:], 0.0))
            made_by(pool.memset(causal[:], 1.0))
            made_by(pool.memset(sel[:], 1.0))
            made_by(pool.iota(time, pattern=[[1, L + 1]], base=0, channel_multiplier=0, allow_small_or_imprecise_dtypes=True))
            made_by(pool.iota(expert_no[:].rearrange("p t e -> p (t e)"), pattern=[[0, T], [1, 8]], base=0, channel_multiplier=0, allow_small_or_imprecise_dtypes=True))
            made_by(pool.iota(part_no[:], pattern=[[0, 1]], base=0, channel_multiplier=1, allow_small_or_imprecise_dtypes=True))
            made_by(pool.iota(par_i[:], pattern=[[0, 2]], base=0, channel_multiplier=1))
            made_by(pool.memset(minus_half[:], -0.5))
            for h in range(H):
                made_by(pool.memset(slope[:, h:h + 1], SLOPES[h]))
            made_by(pool.memset(val[:, :, :, DH], 1.0))
            made_by(pool.memset(nv_pad, 0.0))
            made_by(pool.memset(w1_router[:, E1:8], 0.0))
            made_by(pool.memset(b1_router[:, E1:8], -1e30))
            made_by(pool.memset(row_out[:, 0, :], 0.0))
            pool.wait_ge(pool_made, 3)
            made_by(pool.affine_select(out=ident[:], in_=ident[:], compare_op=ALU.not_equal, fill=1.0, base=0,
                                       pattern=[[-1, P]], channel_multiplier=1))
            made_by(pool.affine_select(out=causal[:], in_=causal[:], compare_op=ALU.is_ge, fill=0.0, base=0,
                                       pattern=[[1, P]], channel_multiplier=-1))
            made_by(pool.affine_select(out=sel[:], in_=sel[:], compare_op=ALU.is_ge, fill=0.0, base=0,
                                       pattern=[[1, HID0]], channel_multiplier=-(HID0 // E0)))
            pool.wait_ge(pool_made, n[0])
            made_by(pool.affine_select(out=sel[:], in_=sel[:], compare_op=ALU.is_ge, fill=0.0, base=HID0 // E0 - 1,
                                       pattern=[[-1, HID0]], channel_multiplier=HID0 // E0))
            assert n[0] == POOL_MADE
            pool.wait_ge(made, MADE_NKSS)
            pool.tensor_tensor(nk_ss[:, 1:2], nk_ss[:, 0:1], minus_half[0:32, 0:1], ALU.pow).then_inc(pool_made, 1)
            pool.wait_ge(pool_made, POOL_MADE + 1)

            def root(norm):
                def step(g):
                    pool.wait_ge(norm.steps.sem, norm.steps.at(g, 9))
                    pool.tensor_tensor(norm.rstd[:], norm.var[:], minus_half[:, 0:4], ALU.pow).then_inc(norm.rooted.sem, 1)
                return step

            def conv_gains(g):
                for k, w in enumerate((conv_a, conv_b)):
                    pool.wait_ge(l_conv.sem, l_conv.at(g, 3 + k))
                    pool.tensor_tensor(conv[:, k, :].rearrange("p (s t) -> p s t", s=SEQ),
                                       conv[:, 2 + k, :].rearrange("p (s t) -> p s t", s=SEQ),
                                       w[:].unsqueeze(1).to_broadcast([P, SEQ, L]), ALU.mult).then_inc(l_gain.sem, 1)

            def keep_x2(g):
                if not first(g):
                    pool.wait_ge(n_o.steps.sem, n_o.steps.at(g - 1))
                pool.wait_ge(n_d.steps.sem, n_d.steps.at(g))
                pool.sem_inc(pool_passed, 1)
                pool.tensor_copy(x2[:], x2n[:]).then_inc(a_kept.sem, 1)
                root(n_a)(g)

            def norms(g, t):
                for k in range(2):
                    pool.wait_ge(a_ss.sem, a_ss.at(g, 6 * t + 3 * (k + 1)))
                    pool.tensor_tensor(rnorm[:, k, t, :], sumsq[:, k, :], minus_half[:], ALU.pow).then_inc(a_root.sem, 1)

            def mask(g, h):
                pool.wait_ge(a_exp.sem, a_exp.at(g, 2 * h + 1))
                pd = rows3(p_diag[:, h % 2, :])
                pool.tensor_tensor(pd, pd, causal[:].unsqueeze(1).to_broadcast([P, T, P]), ALU.mult).then_inc(a_mask.sem, 1)

            def ce_residual(g):
                root(n_c)(g)

            def ce_residual2(g):
                pool.wait_ge(n_c.steps.sem, n_c.steps.at(g))
                pool.tensor_tensor(ce_res, ce_rows, row_g1[:].unsqueeze(1).to_broadcast([P, T, D]), ALU.mult).then_inc(f_res.sem, 1)
                pool.wait_ge(f_res.sem, f_res.at(g, 1))
                pool.tensor_tensor(ce_res, ce_res, row_res[:].unsqueeze(1).to_broadcast([P, T, D]), ALU.add).then_inc(f_res.sem, 1)

            def weigh(g, t):
                pool.wait_ge(f_eb.sem, f_eb.at(g, 2 * t + 1))
                pool.tensor_tensor(mix_e, mix_e, pick1[:, 0, t, 0:E1].unsqueeze(2).to_broadcast([P, E1, D]),
                                   ALU.mult).then_inc(f_ew.sem, 1)

            plan(pool, {
                "l_stats": root(n_x), "l_scan": conv_gains, "l_back": root(n_y), "l_res": root(n_l), "l_down": root(n_d),
                "a_stats": keep_x2, "a_proj": norms, "a_scores": mask, "a_out": root(n_o),
                "f_stats": root(n_m), "f_ce": ce_residual, "f_ce_apply": ce_residual2, "f_ce2": root(n_c2),
                "f_out": weigh, "f_end_stats": root(n_f),
            })

        @block.scalar
        def _(act):
            n = [0]

            def made_by(i):
                n[0] += 1
                i.then_inc(act_made, 1)

            act.wait_ge(loaded0, 16 * 7)
            made_by(act.activation(col["decay"], col["lnabs"], ACT.Exp))
            act.wait_ge(made, 3)
            made_by(act.activation(col["r"], col["nz"], ACT.Exp))
            act.wait_ge(pool_made, POOL_MADE)
            made_by(act.activation(rpow, time, ACT.Exp, scale=col["nz"]))
            assert n[0] == 3
            act.wait_ge(made, MADE_FRAC)
            made_by(act.activation(sin_t[:], part_a, ACT.Sin, scale=TWO_PI))
            made_by(act.activation(cos_t[:], part_b, ACT.Sin, scale=TWO_PI))
            for k in range(4):
                act.wait_ge(pe_made, k + 1)
                if k == 0:
                    made_by(act.activation(nk_zT, bank[0][:, 0:32], ACT.Copy))
                    made_by(act.activation(nv_zT, bank[0][:, 32:64], ACT.Copy))
                elif k == 1:
                    made_by(act.activation(wqT[:, 0:4, :], bank[1][:].rearrange("p (c n) -> p c n", n=P), ACT.Copy))
                elif k == 2:
                    made_by(act.activation(wqT[:, 4:8, :], bank[2][:].rearrange("p (c n) -> p c n", n=P), ACT.Copy))
                else:
                    for i in range(3):
                        made_by(act.activation(wT[i], bank[3][:, 128 * i:128 * i + 128], ACT.Copy))
            act.wait_ge(pe_made, 5)
            for i in range(2):
                made_by(act.activation(wT[4 + i], bank[4][:, 128 * i:128 * i + 128], ACT.Copy))
            act.wait_ge(pe_made, 7)
            made_by(act.activation(me_p1, bank[0][:, 0:256], ACT.Copy))
            act.wait_ge(pe_made, 8)
            made_by(act.activation(me_p2, bank[1][:, 0:256], ACT.Copy))
            act.wait_ge(pe_made, 9)
            made_by(act.activation(w_me[:], bank[0][:, 0:256], ACT.Copy))
            assert n[0] == ACT_MADE
            act.wait_ge(act_made, ACT_MADE)

            def to_cols(g):
                act.wait_ge(l_turned.sem, l_turned.at(g, 3))
                act.activation(xlT[:], bank[6][:], ACT.Copy).then_inc(l_cols.sem, 1)

            def exps0(g):
                act.wait_ge(l_pick.sem, l_pick.at(g, 2 + 2 * T))
                act.activation(exp0[:], exp0[:], ACT.Exp).then_inc(l_exp.sem, 1)

            def coef_cols(g):
                act.wait_ge(l_routed.sem, l_routed.at(g, 2))
                act.activation(coef0T[:], bank[7][0:E0, :], ACT.Copy).then_inc(l_cols.sem, 1)

            def tanh_l(g, j):
                act.wait_ge(l_gu.sem, l_gu.at(g, j + 1))
                act.activation(tanh0[:], bank[4][:], ACT.Tanh, scale=0.5).then_inc(l_tanh.sem, 1)

            def a_apply(g):
                act.wait_ge(a_turned.sem, a_turned.at(g))
                act.activation(xaT[:], bank[0][:], ACT.Copy).then_inc(a_cols.sem, 1)

            ITEM_BANK = (2, 3, 0, 1)

            def squares(g, t):
                for k in range(4):
                    act.wait_ge(a_proj.sem, a_proj.at(g, 4 * t + k + 1))
                    if k >= 2:
                        act.wait_ge(a_ss.sem, a_ss.at(g, 6 * t + k - 1))
                    elif t:
                        act.wait_ge(a_ss.sem, a_ss.at(g, 6 * t - 2 + k))
                    elif not first(g):
                        act.wait_ge(a_ss.sem, a_ss.at(g - 1, 6 * T - 2 + k))
                    act.activation(square[:, k % 2, :], bank[ITEM_BANK[k]][:], ACT.Square).then_inc(a_sq.sem, 1)

            def flat(g, t):
                for k in range(4):
                    act.wait_ge(a_turn.sem, a_turn.at(g, 4 * t + k + 1))
                    dst = (kT, kT, qT, qT)[k][:, 4 * (k % 2):4 * (k % 2) + 4, t * P:(t + 1) * P]
                    src = bank[ITEM_BANK[k]][:].rearrange("p (c n) -> p c n", n=P)
                    if k < 2:
                        act.activation(dst, src, ACT.Copy).then_inc(a_flat.sem, 1)
                    else:
                        act.activation(dst, src, ACT.Copy, scale=qk_scale[:]).then_inc(a_flat.sem, 1)

            def values(g, t):
                for k in range(2):
                    act.wait_ge(a_v.sem, a_v.at(g, 2 * t + k + 1))
                    act.activation(val[:, t, 8 * k:8 * k + 8, 0:DH], bank[k][:].rearrange("p (h d) -> p h d", d=DH),
                                   ACT.Copy).then_inc(a_vals.sem, 1)

            def null_exps(g):
                act.wait_ge(a_nullc.sem, a_nullc.at(g, 3))
                act.activation(null_p[:], null_s[:], ACT.Exp).then_inc(a_nexp.sem, 1)

            def score_exps(g, h):
                if h >= 2:
                    act.wait_ge(a_pv.sem, a_pv.at(g, h - 1))
                act.wait_ge(a_s.sem, a_s.at(g, 2 * h + 1))
                act.activation(p_diag[:, h % 2, :], bank[h % 2][:], ACT.Exp, bias=bias_diag[:, h:h + 1],
                               scale=8.0).then_inc(a_exp.sem, 1)
                act.wait_ge(a_s.sem, a_s.at(g, 2 * h + 2))
                act.activation(p_off[:, h % 2, :], bank[2][:, 0:2 * P], ACT.Exp, bias=bias_off[:, h:h + 1],
                               scale=8.0).then_inc(a_exp.sem, 1)

            def out_cols(g):
                act.wait_ge(a_oT.sem, a_oT.at(g, 1))
                act.activation(null_pT[:], bank[3][0:H * NULLS, :], ACT.Copy).then_inc(a_oc.sem, 1)
                for c in range(8):
                    act.wait_ge(a_oT.sem, a_oT.at(g, c + 2))
                    act.activation(outT[:, c, :], bank[c % 3][:], ACT.Copy).then_inc(a_oc.sem, 1)

            def f_apply(g):
                act.wait_ge(f_turned.sem, f_turned.at(g))
                act.activation(xmT[:], bank[4][:], ACT.Copy).then_inc(f_cols.sem, 1)

            def f_route(g):
                act.wait_ge(f_pick.sem, f_pick.at(g, 2 + 2 * T))
                act.activation(gap1[:], gap1[:], ACT.Tanh, scale=0.5).then_inc(f_gap.sem, 1)

            def f_sw(g, j):
                act.wait_ge(f_gu.sem, f_gu.at(g, j + 1))
                act.activation(tanh1, bank[4][:], ACT.Tanh, scale=0.5).then_inc(f_tanh.sem, 1)

            def f_me_(g, j):
                act.wait_ge(f_me.sem, f_me.at(g, j + 1))
                act.activation(hid_me[j], bank[7][:], ACT.Gelu, bias=b_me[:, j:j + 1]).then_inc(f_meg.sem, 1)

            def f_ml_(g, j):
                act.wait_ge(f_ml.sem, f_ml.at(g, j + 1))
                act.activation(hid_ml[j], bank[4 + j % 2][:], ACT.Gelu, bias=b_ml[:, j:j + 1]).then_inc(f_mlg.sem, 1)

            def f_ce_apply(g):
                act.wait_ge(f_ce.sem, f_ce.at(g, 2))
                act.activation(ce_T, bank[6][:], ACT.Copy).then_inc(f_cec.sem, 1)

            def f_relu_(g, j):
                act.wait_ge(f_r.sem, f_r.at(g, j + 1))
                act.activation(hid_relu[j], bank[6 + j][:], ACT.Relu, bias=b_f1[:, j:j + 1]).then_inc(f_relu.sem, 1)

            def f_ce2_apply(g):
                act.wait_ge(f_gT.sem, f_gT.at(g))
                act.activation(ce_T, bank[6][:], ACT.Copy).then_inc(f_cec.sem, 1)

            plan(act, {
                "l_norm": to_cols, "l_route": exps0, "l_coef": coef_cols, "l_chunk": tanh_l,
                "a_apply": a_apply, "a_proj": squares, "a_turn": flat, "a_value": values, "a_nexp": null_exps,
                "a_scores": score_exps, "a_oT": out_cols,
                "f_apply": f_apply, "f_pick": f_route, "f_sw": f_sw, "f_me": f_me_, "f_ml": f_ml_,
                "f_ce_apply": f_ce_apply, "f_relu": f_relu_, "f_ce2_apply": f_ce2_apply,
            })

        @block.vector
        def _(dve):
            n = [0]

            def link(i):
                n[0] += 1
                i.then_inc(made, 1)
                dve.wait_ge(made, n[0])

            V = nc.vector
            dve.wait_ge(act_made, 1)
            link(V.tensor_tensor(col["z"], col["decay"], col["scale"], ALU.mult))
            link(V.tensor_scalar(col["nz"], col["z"], -1.0, None, ALU.mult))
            link(V.tensor_tensor(col["theta"], col["angle"], col["scale"], ALU.mult))
            dve.wait_ge(pool_made, POOL_MADE)
            link(V.tensor_scalar(phase, time, col["theta"], 1.0 / TWO_PI, ALU.mult, ALU.mult))
            for shift, dst in ((0.0, part_a), (0.25, part_b)):
                link(V.tensor_scalar(frac, phase, shift, None, ALU.add))
                link(V.tensor_scalar(turns, frac, ROUND, None, ALU.add))
                link(V.tensor_scalar(turns, turns, -ROUND, None, ALU.add))
                link(V.tensor_tensor(frac, frac, turns, ALU.subtract))
                link(V.tensor_scalar(dst, frac, 0.4999999, -0.4999999, ALU.min, ALU.max))
            assert n[0] == MADE_FRAC
            dve.wait_ge(act_made, 5)
            link(V.tensor_scalar(col["gate"], col["r"], -1.0, 1.0, ALU.mult, ALU.add))
            c0, s0 = cos_t[:, 0:L], sin_t[:, 0:L]
            link(V.tensor_scalar(part_a[:, 0:L], s0, col["init_im"], None, ALU.mult))
            link(V.scalar_tensor_tensor(out=part_a[:, 0:L], in0=c0, scalar=col["init_re"], in1=part_a[:, 0:L], op0=ALU.mult, op1=ALU.subtract))
            link(V.tensor_scalar(conv_a[:], part_a[:, 0:L], col["gate"], None, ALU.mult))
            link(V.tensor_scalar(part_b[:, 0:L], c0, col["init_im"], None, ALU.mult))
            link(V.scalar_tensor_tensor(out=part_b[:, 0:L], in0=s0, scalar=col["init_re"], in1=part_b[:, 0:L], op0=ALU.mult, op1=ALU.add))
            link(V.tensor_scalar(conv_b[:], part_b[:, 0:L], col["gate"], None, ALU.mult))
            c1, s1 = cos_t[:, 1:L + 1], sin_t[:, 1:L + 1]
            link(V.tensor_scalar(part_a[:, 0:L], s1, col["last_im"], None, ALU.mult))
            link(V.scalar_tensor_tensor(out=part_a[:, 0:L], in0=c1, scalar=col["last_re"], in1=part_a[:, 0:L], op0=ALU.mult, op1=ALU.subtract))
            link(V.tensor_tensor(part_a[:, 0:L], part_a[:, 0:L], rpow[:, 1:L + 1], ALU.mult))
            link(V.tensor_scalar(conv_c[:], part_a[:, 0:L], col["gate"], None, ALU.mult))
            dr = decay_row[:].rearrange("p (s t) -> p s t", s=SEQ)
            link(V.tensor_scalar(dr, time[:, 0:L].unsqueeze(1).to_broadcast([P, SEQ, L]), 0.0, col["r"], ALU.mult, ALU.add))
            link(V.memset(dr[:, :, 0:1], 0.0))
            link(V.memset(zero_col[:], 0.0))
            link(V.tensor_scalar(zraw[:, 0:1], part_no[:], -float(MID), None, ALU.add))
            link(V.tensor_scalar(zraw[:, 1:2], part_no[:], -float(MID + P), None, ALU.add))
            link(V.tensor_scalar(bias_diag[:], slope[:], zraw[:, 0:1], None, ALU.mult))
            link(V.tensor_scalar(bias_off[:], slope[:], zraw[:, 1:2], None, ALU.mult))
            for t in range(T):
                for k in range(NULLS):
                    link(V.tensor_scalar(bias_null[:, t, :, k], slope[:], float(k - NULLS - MID - P * (t % 2)), None, ALU.mult))
            dve.wait_ge(loaded1, 16 * 7)
            link(V.tensor_scalar(w0_down[:], w0_down[:], 0.5, None, ALU.mult))
            dve.wait_ge(loaded2, 16 * LOADS2)
            link(V.tensor_scalar(w_sw2[:], w_sw2[:], 0.5, None, ALU.mult))
            link(V.tensor_scalar(w_q[:], w_q[:], col["gamma"], None, ALU.mult))
            link(V.tensor_scalar(w_kv[:], w_kv[:], col["gamma"], None, ALU.mult))
            link(V.tensor_tensor(qk_scale[:], col["qs"], col["ks"], ALU.mult))
            link(V.tensor_tensor(b1_router[:, 0:E1], b1_router[:, 0:E1], lb_row[:, 0:E1], ALU.add))
            link(V.tensor_tensor(qs_row, qs_row, ks_row, ALU.mult))
            link(V.tensor_tensor(nk_sq, nk_rows, nk_rows, ALU.mult))
            link(V.tensor_reduce(nk_ss[:, 0:1], nk_sq, AX_X, ALU.add))
            link(V.tensor_scalar(nk_ss[:, 0:1], nk_ss[:, 0:1], 1e-24, None, ALU.max))
            assert n[0] == MADE_NKSS, n[0]
            link(V.tensor_scalar(par_i[:], par_i[:], 1, 1, ALU.logical_shift_right, ALU.bitwise_and))
            link(V.tensor_copy(par[:, 1:2], par_i[:, 0:1]))
            link(V.tensor_scalar(par[:, 0:1], par[:, 1:2], -1.0, 1.0, ALU.mult, ALU.add))
            dve.wait_ge(pool_made, POOL_MADE + 1)
            link(V.tensor_scalar(nk_rows, nk_rows, nk_ss[:, 1:2], None, ALU.mult))
            link(V.tensor_tensor(nk_rows, nk_rows, qs_row, ALU.mult))
            for s in range(2):
                link(V.tensor_scalar(nk_z[:, 64 * s:64 * s + 64], nk_rows, par[:, s:s + 1], None, ALU.mult))
                link(V.tensor_scalar(nv_z[:, 64 * s:64 * s + 64], nv_rows, par[:, s:s + 1], None, ALU.mult))
            link(V.tensor_copy(colb[0], col["syn_b"].to_broadcast([P, P])))
            link(V.tensor_copy(colb[1], col["ce_bv"].to_broadcast([P, P])))
            link(V.tensor_copy(colb[2], col["n2b"].to_broadcast([P, P])))
            assert n[0] == MADE_RAW, n[0]
            dve.wait_ge(act_made, 7)
            for c in range(8):
                link(V.tensor_copy(nv_pad[:, c, 4 * c:4 * c + 4], nv_zT[:, 4 * c:4 * c + 4]))
            assert n[0] == MADE_PAD
            dve.wait_ge(pe_made, 6)
            link(V.tensor_tensor(ce_v2, bank[5][:, 0:P], ident[:], ALU.add))
            assert n[0] == MADE_V2
            dve.wait_ge(pe_made, 10)
            link(V.tensor_copy(w_ce[:], bank[2][:, 0:P]))
            link(V.tensor_tensor(row_ce[:], bank[2][:, P:2 * P], row_tmp[0], ALU.add))
            link(V.tensor_tensor(row_out[:, 2, :], bank[2][:, 2 * P:3 * P], row_tmp[2], ALU.add))
            link(V.tensor_tensor(row_res[:], row_tmp[1], row_tmp[3], ALU.add))
            link(V.tensor_tensor(b_me[:], bank[3][:, 0:2], c1b, ALU.add))
            link(V.tensor_tensor(b_f1[:], bank[3][:, 2:4], f1b, ALU.add))
            link(V.tensor_copy(w_nk[:], bank[3][:, 8:8 + H * NULLS]))
            link(V.tensor_copy(w_nv[:], bank[4][0:H * NULLS, 256:256 + P]))
            link(V.tensor_scalar(w_f1[:], w_f1[:], col["n1g"], None, ALU.mult))
            link(V.tensor_scalar(w_gen[:], w_gen[:], col["n2g"], None, ALU.mult))
            dve.wait_ge(act_made, ACT_MADE)
            V.memset(zero_col[:], 0.0).then_inc(all_set, 1)
            dve.wait_ge(all_set, 1)

            def stats(norm, g, tile):
                s = norm.steps
                for t in range(T):
                    V.bn_stats(norm.six[:, t, :], tile(t)).then_inc(s.sem, 1)
                dve.wait_ge(s.sem, s.at(g, 4))
                dve.sem_inc(dve_passed, 1)
                for t in range(T):
                    V.bn_aggr(norm.mv[:, t, :], norm.six[:, t, :]).then_inc(s.sem, 1)
                dve.wait_ge(s.sem, s.at(g, 8))
                V.tensor_scalar(norm.var[:], norm.mv[:, :, 1], norm.scale, norm.add, ALU.mult, ALU.add).then_inc(s.sem, 1)

            def apply(norm, g, dst, tile):
                dve.wait_ge(norm.rooted.sem, norm.rooted.at(g))
                for t in range(T):
                    V.tensor_scalar(dst[:, t, :], tile(t), norm.mv[:, t, 0:1], norm.rstd[:, t:t + 1],
                                    ALU.subtract, ALU.mult).then_inc(norm.steps.sem, 1)

            def add_residual(norm, g, dst, normed, res):
                dve.wait_ge(norm.steps.sem, norm.steps.at(g, 13))
                V.tensor_tensor(dst[:], normed[:], res[:], ALU.add).then_inc(norm.steps.sem, 1)

            def l_stats(g):
                dve.wait_ge(x_loaded.sem, x_loaded.at(g))
                stats(n_x, g, lambda t: xin[:, t, :])

            def l_apply(g):
                apply(n_x, g, xn, lambda t: xin[:, t, :])
                dve.wait_ge(l_turned.sem, l_turned.at(g, 1))
                for k, w in enumerate((cos_t, sin_t)):
                    V.tensor_tensor(conv[:, k, :].rearrange("p (s t) -> p s t", s=SEQ),
                                    bank[6][:].rearrange("p (s t) -> p s t", s=SEQ),
                                    w[:, 0:L].unsqueeze(1).to_broadcast([P, SEQ, L]), ALU.mult).then_inc(l_conv.sem, 1)
                for k in range(2):
                    dve.wait_ge(l_conv.sem, l_conv.at(g, 1 + k))
                    V.tensor_tensor_scan(conv[:, 2 + k, :], decay_row[:], conv[:, k, :], 0.0, ALU.mult, ALU.add).then_inc(l_conv.sem, 1)

            def l_back(g):
                dve.wait_ge(l_gain.sem, l_gain.at(g))
                V.tensor_tensor(conv[:, 0, :], conv[:, 0, :], conv[:, 1, :], ALU.add).then_inc(l_conv.sem, 1)
                dve.wait_ge(l_conv.sem, l_conv.at(g, 5))
                V.tensor_tensor(conv[:, 0, :].rearrange("p (s t) -> p s t", s=SEQ),
                                conv[:, 0, :].rearrange("p (s t) -> p s t", s=SEQ),
                                conv_c[:].unsqueeze(1).to_broadcast([P, SEQ, L]), ALU.add).then_inc(l_conv.sem, 1)
                dve.wait_ge(l_turned.sem, l_turned.at(g, 2))
                stats(n_y, g, lambda t: bank[6][:, t * P:(t + 1) * P])

            def l_res(g):
                apply(n_y, g, xn, lambda t: bank[6][:, t * P:(t + 1) * P])
                add_residual(n_y, g, x1, xn, xin)
                dve.wait_ge(n_y.steps.sem, n_y.steps.at(g))
                stats(n_l, g, lambda t: x1[:, t, :])

            def l_norm(g):
                apply(n_l, g, xn, lambda t: x1[:, t, :])

            def l_route(g):
                s = l_pick
                dve.wait_ge(l_routed.sem, l_routed.at(g, 1))
                V.tensor_copy(logit0[:], bank[7][:, 0:T * 8].rearrange("p (t e) -> p t e", e=8)).then_inc(s.sem, 1)
                dve.wait_ge(s.sem, s.at(g, 1))
                dve.sem_inc(dve_passed, 1)
                for t in range(T):
                    V.max(top0[:, t, :], logit0[:, t, :]).then_inc(s.sem, 1)
                dve.wait_ge(s.sem, s.at(g, 1 + T))
                dve.sem_inc(dve_passed, 1)
                for t in range(T):
                    V.max_index(idx0[:, t, :], top0[:, t, :], logit0[:, t, :]).then_inc(s.sem, 1)
                V.tensor_tensor(exp0[:], top0[:], top0[:, :, 0:1].to_broadcast([P, T, 8]), ALU.subtract).then_inc(s.sem, 1)

            def l_coef(g):
                s = l_pick
                k = 2 + 2 * T
                dve.wait_ge(s.sem, s.at(g, k))
                V.tensor_copy(idf0[:], idx0[:, :, 0:2]).then_inc(s.sem, 1)
                dve.wait_ge(l_exp.sem, l_exp.at(g))
                V.tensor_reduce(sum0[:], exp0[:], AX_X, ALU.add).then_inc(s.sem, 1)
                dve.wait_ge(s.sem, s.at(g, k + 2))
                V.reciprocal(sum0[:], sum0[:]).then_inc(s.sem, 1)
                for j in range(2):
                    V.tensor_tensor(pick0[:, j, :, :], expert_no[:], idf0[:, :, j:j + 1].to_broadcast([P, T, 8]), ALU.is_equal).then_inc(s.sem, 1)
                dve.wait_ge(s.sem, s.at(g, k + 3))
                V.tensor_tensor(prob0[:], exp0[:, :, 0:2], sum0[:].unsqueeze(2).to_broadcast([P, T, 2]), ALU.mult).then_inc(s.sem, 1)
                dve.wait_ge(s.sem, s.at(g, k + 6))
                for j in range(2):
                    V.tensor_tensor(pick0[:, j, :, :], pick0[:, j, :, :], prob0[:, :, j:j + 1].to_broadcast([P, T, 8]), ALU.mult).then_inc(s.sem, 1)
                dve.wait_ge(s.sem, s.at(g, k + 8))
                V.tensor_tensor(pick0[:, 0, :, :], pick0[:, 0, :, :], pick0[:, 1, :, :], ALU.add).then_inc(l_coefd.sem, 1)

            def l_chunk(g, j):
                s = l_hid
                b = 3 * j
                dve.wait_ge(l_tanh.sem, l_tanh.at(g, j + 1))
                V.scalar_tensor_tensor(out=hid0[:, j, :], in0=tanh0[:], scalar=1.0, in1=bank[4][:], op0=ALU.add, op1=ALU.mult).then_inc(s.sem, 1)
                dve.wait_ge(s.sem, s.at(g, b + 1))
                V.tensor_tensor(hid0[:, j, :], hid0[:, j, :], bank[5][:], ALU.mult).then_inc(s.sem, 1)
                if j < J0:
                    dve.wait_ge(s.sem, s.at(g, b + 2))
                    V.tensor_tensor(hid0[:, j, :], hid0[:, j, :], bank[6][:], ALU.mult).then_inc(s.sem, 1)

            def l_down_(g):
                dve.wait_ge(l_down.sem, l_down.at(g))
                stats(n_d, g, lambda t: bank[7][:, t * P:(t + 1) * P])

            def l_end(g):
                apply(n_d, g, xn, lambda t: bank[7][:, t * P:(t + 1) * P])
                if not first(g):
                    dve.wait_ge(a_kept.sem, a_kept.at(g - 1))
                add_residual(n_d, g, x2n, xn, x1)

            def a_stats(g):
                dve.wait_ge(n_d.steps.sem, n_d.steps.at(g))
                stats(n_a, g, lambda t: x2n[:, t, :])

            def a_apply(g):
                apply(n_a, g, xa, lambda t: x2n[:, t, :])

            def a_null(g):
                dve.wait_ge(a_nulls.sem, a_nulls.at(g))
                V.tensor_copy(null_s[:], bank[3][:, 0:T * H * NULLS].rearrange("p (t h n) -> p t h n", h=H, n=NULLS)).then_inc(a_nullc.sem, 1)

            def a_sums(g, t):
                s = a_ss
                for k in range(2):
                    for j in range(2):
                        dve.wait_ge(a_sq.sem, a_sq.at(g, 4 * t + 2 * k + j + 1))
                        if j == 0 and (t or not first(g)):
                            dve.wait_ge(a_root.sem, a_root.at(g, 2 * t + k - 1))
                        V.tensor_reduce(sumsq[:, k, 8 * j:8 * j + 8], square[:, j, :].rearrange("p (h d) -> p h d", d=DH),
                                        AX_X, ALU.add).then_inc(s.sem, 1)
                    dve.wait_ge(s.sem, s.at(g, 6 * t + 3 * k + 2))
                    V.tensor_scalar(sumsq[:, k, :], sumsq[:, k, :], 1e-24, None, ALU.max).then_inc(s.sem, 1)

            ITEM_BANK = (2, 3, 0, 1)

            def a_units(g, t):
                for k in range(4):
                    dve.wait_ge(a_root.sem, a_root.at(g, 2 * t + k // 2 + 1))
                    V.tensor_tensor(unit[:, k, :].rearrange("p (h d) -> p h d", d=DH),
                                    bank[ITEM_BANK[k]][:].rearrange("p (h d) -> p h d", d=DH),
                                    rnorm[:, k // 2, t, 8 * (k % 2):8 * (k % 2) + 8].unsqueeze(2).to_broadcast([P, 8, DH]),
                                    ALU.mult).then_inc(a_unit.sem, 1)

            def a_nexp_(g):
                dve.wait_ge(a_nullc.sem, a_nullc.at(g, 1))
                V.tensor_tensor(null_s[:], null_s[:], rnorm[:, 1, :, :].unsqueeze(3).to_broadcast([P, T, H, NULLS]), ALU.mult).then_inc(a_nullc.sem, 1)
                dve.wait_ge(a_nullc.sem, a_nullc.at(g, 2))
                V.scalar_tensor_tensor(out=null_s[:].rearrange("p t h n -> p (t h n)"), in0=null_s[:].rearrange("p t h n -> p (t h n)"),
                                       scalar=8.0, in1=bias_null[:].rearrange("p t h n -> p (t h n)"),
                                       op0=ALU.mult, op1=ALU.add).then_inc(a_nullc.sem, 1)
                dve.wait_ge(a_nexp.sem, a_nexp.at(g))
                V.tensor_tensor(null_sum[:], null_p[:, :, :, 0], null_p[:, :, :, 1], ALU.add).then_inc(a_nullc.sem, 1)

            def a_mixes(g, h):
                s = a_mix
                pv = bank[3][:, 0:T * (DH + 1)].rearrange("p (t d) -> p t d", t=T)
                dve.wait_ge(a_pv.sem, a_pv.at(g, h + 1))
                if h == 0:
                    dve.wait_ge(a_nullc.sem, a_nullc.at(g, 4))
                V.tensor_tensor(denom[:], pv[:, :, DH], null_sum[:, :, h], ALU.add).then_inc(s.sem, 1)
                dve.wait_ge(s.sem, s.at(g, 3 * h + 1))
                V.reciprocal(recip[:, :, h], denom[:]).then_inc(s.sem, 1)
                dve.wait_ge(s.sem, s.at(g, 3 * h + 2))
                V.tensor_tensor(mixed[:, :, h * DH:(h + 1) * DH], pv[:, :, 0:DH],
                                recip[:, :, h:h + 1].to_broadcast([P, T, DH]), ALU.mult).then_inc(s.sem, 1)
                if h == H - 1:
                    V.tensor_tensor(null_p[:], null_p[:], recip[:].unsqueeze(3).to_broadcast([P, T, H, NULLS]), ALU.mult).then_inc(a_pn.sem, 1)

            def a_out_(g):
                dve.wait_ge(a_out.sem, a_out.at(g))
                stats(n_o, g, lambda t: bank[3][:, t * P:(t + 1) * P])

            def a_end(g):
                apply(n_o, g, xa, lambda t: bank[3][:, t * P:(t + 1) * P])
                dve.wait_ge(a_kept.sem, a_kept.at(g))
                add_residual(n_o, g, x3, xa, x2)

            def f_stats(g):
                dve.wait_ge(n_o.steps.sem, n_o.steps.at(g))
                stats(n_m, g, lambda t: x3[:, t, :])

            def f_apply(g):
                apply(n_m, g, x4m, lambda t: x3[:, t, :])

            def f_ce_(g):
                dve.wait_ge(f_ce.sem, f_ce.at(g, 1))
                V.tensor_tensor(ce_rows, rows3(bank[6][:]), row_ce[:].unsqueeze(1).to_broadcast([P, T, D]), ALU.add).then_inc(f_ced.sem, 1)
                dve.wait_ge(f_ced.sem, f_ced.at(g, 1))
                stats(n_c, g, lambda t: ce_rows[:, t, :])

            def f_ce_apply(g):
                apply(n_c, g, ce_rows, lambda t: ce_rows[:, t, :])

            def f_ce2(g):
                dve.wait_ge(f_ce.sem, f_ce.at(g, 3))
                dve.wait_ge(f_res.sem, f_res.at(g))
                V.tensor_tensor(ce_rows, rows3(bank[6][:]), ce_res, ALU.add).then_inc(f_ced.sem, 1)
                dve.wait_ge(f_ced.sem, f_ced.at(g, 2))
                stats(n_c2, g, lambda t: ce_rows[:, t, :])

            def f_ce2_apply(g):
                apply(n_c2, g, ce_rows, lambda t: ce_rows[:, t, :])

            def f_route(g):
                s = f_pick
                dve.wait_ge(f_routed.sem, f_routed.at(g))
                V.tensor_tensor(logit1[:], bank[7][:, 0:T * 8].rearrange("p (t e) -> p t e", e=8),
                                b1_router[:].unsqueeze(1).to_broadcast([P, T, 8]), ALU.add).then_inc(s.sem, 1)
                dve.wait_ge(s.sem, s.at(g, 1))
                dve.sem_inc(dve_passed, 1)
                for t in range(T):
                    V.max(top1[:, t, :], logit1[:, t, :]).then_inc(s.sem, 1)
                dve.wait_ge(s.sem, s.at(g, 1 + T))
                dve.sem_inc(dve_passed, 1)
                for t in range(T):
                    V.max_index(idx1[:, t, :], top1[:, t, :], logit1[:, t, :]).then_inc(s.sem, 1)
                V.tensor_tensor(gap1[:], top1[:, :, 1], top1[:, :, 0], ALU.subtract).then_inc(s.sem, 1)

            def f_pick_(g):
                s = f_pick
                k = 2 + 2 * T
                dve.wait_ge(s.sem, s.at(g, k))
                V.tensor_copy(idf1[:], idx1[:, :, 0:2]).then_inc(s.sem, 1)
                dve.wait_ge(f_gap.sem, f_gap.at(g))
                V.tensor_scalar(wt1[:, :, 0], gap1[:], -0.5, 0.5, ALU.mult, ALU.add).then_inc(s.sem, 1)
                V.tensor_scalar(wt1[:, :, 1], gap1[:], 0.5, 0.5, ALU.mult, ALU.add).then_inc(s.sem, 1)
                dve.wait_ge(s.sem, s.at(g, k + 1))
                for j in range(2):
                    V.tensor_tensor(pick1[:, j, :, :], expert_no[:], idf1[:, :, j:j + 1].to_broadcast([P, T, 8]), ALU.is_equal).then_inc(s.sem, 1)
                dve.wait_ge(s.sem, s.at(g, k + 5))
                for j in range(2):
                    V.tensor_tensor(pick1[:, j, :, :], pick1[:, j, :, :], wt1[:, :, j:j + 1].to_broadcast([P, T, 8]), ALU.mult).then_inc(s.sem, 1)
                dve.wait_ge(s.sem, s.at(g, k + 7))
                V.tensor_tensor(pick1[:, 0, :, :], pick1[:, 0, :, :], pick1[:, 1, :, :], ALU.add).then_inc(f_coefd.sem, 1)

            def f_sw(g, j):
                s = f_hid
                dve.wait_ge(f_tanh.sem, f_tanh.at(g, j + 1))
                V.scalar_tensor_tensor(out=hid_sw[j], in0=tanh1, scalar=1.0, in1=bank[4][:], op0=ALU.add, op1=ALU.mult).then_inc(s.sem, 1)
                dve.wait_ge(s.sem, s.at(g, 2 * j + 1))
                V.tensor_tensor(hid_sw[j], hid_sw[j], bank[5][:], ALU.mult).then_inc(s.sem, 1)

            def f_out(g, t):
                dve.wait_ge(f_e.sem, f_e.at(g, t + 1))
                if t:
                    dve.wait_ge(f_eb.sem, f_eb.at(g, 2 * t))
                V.tensor_tensor(mix_e, bank[4 + t][:].rearrange("p (e d) -> p e d", e=E1), row_out[:], ALU.add).then_inc(f_eb.sem, 1)
                dve.wait_ge(f_ew.sem, f_ew.at(g, t + 1))
                V.tensor_reduce(x4m[:, t, :], mix_e.rearrange("p e d -> p d e"), AX_X, ALU.add).then_inc(f_eb.sem, 1)

            def f_end_stats(g):
                dve.wait_ge(f_eb.sem, f_eb.at(g))
                stats(n_f, g, lambda t: x4m[:, t, :])

            def f_end(g):
                apply(n_f, g, x4m, lambda t: x4m[:, t, :])
                dve.wait_ge(stored.sem, stored.at(g))
                add_residual(n_f, g, x4, x4m, x3)

            plan(dve, {
                "l_stats": l_stats, "l_apply": l_apply, "l_back": l_back, "l_res": l_res, "l_norm": l_norm,
                "l_route": l_route, "l_coef": l_coef, "l_chunk": l_chunk, "l_down": l_down_, "l_end": l_end,
                "a_stats": a_stats, "a_apply": a_apply, "a_null": a_null, "a_proj": a_sums, "a_turn": a_units,
                "a_nexp": a_nexp_, "a_mix": a_mixes, "a_out": a_out_, "a_end": a_end,
                "f_stats": f_stats, "f_apply": f_apply, "f_route": f_route, "f_pick": f_pick_, "f_ce": f_ce_,
                "f_ce_apply": f_ce_apply, "f_ce2": f_ce2, "f_ce2_apply": f_ce2_apply, "f_sw": f_sw, "f_out": f_out,
                "f_end_stats": f_end_stats, "f_end": f_end,
            })

        @block.tensor
        def _(pe):
            mm = nc.tensor.matmul

            def turn(dst, src):
                for t in range(4):
                    last = nc.tensor.transpose(dst[:, t * P:(t + 1) * P], src(t), ident[:])
                return last

            pe.wait_ge(pool_made, POOL_MADE)
            pe.wait_ge(made, MADE_RAW)
            nc.tensor.transpose(bank[0][:, 0:32], nk_z, ident[0:32, 0:32])
            nc.tensor.transpose(bank[0][:, 32:64], nv_z, ident[0:32, 0:32]).then_inc(pe_made, 1)
            turn(bank[1], lambda t: w_q[:, t * P:(t + 1) * P]).then_inc(pe_made, 1)
            turn(bank[2], lambda t: w_q[:, (4 + t) * P:(5 + t) * P]).then_inc(pe_made, 1)
            for i in range(3):
                last = nc.tensor.transpose(bank[3][:, i * P:(i + 1) * P], me_raw[i], ident[:])
            last.then_inc(pe_made, 1)
            for i in range(2):
                last = nc.tensor.transpose(bank[4][:, i * P:(i + 1) * P], ce_raw[i], ident[:])
            last.then_inc(pe_made, 1)
            pe.wait_ge(act_made, 14)
            mm(bank[5][:, 0:P], wT[5], ce_raw[2], start=True, stop=True).then_inc(pe_made, 1)
            mm(bank[0][:, 0:2 * P], wT[2], me_c1, start=True, stop=True).then_inc(pe_made, 1)
            pe.wait_ge(act_made, 15)
            mm(bank[1][:, 0:2 * P], wT[1], me_p1, start=True, stop=True).then_inc(pe_made, 1)
            pe.wait_ge(act_made, 16)
            mm(bank[0][:, 0:2 * P], wT[0], me_p2, start=True, stop=True).then_inc(pe_made, 1)
            pe.wait_ge(made, MADE_V2)
            mm(bank[2][:, 0:P], wT[4], ce_v2, start=True, stop=True)
            mm(bank[2][:, P:2 * P], colb[0], ce_v2, start=True, stop=False)
            mm(bank[2][:, P:2 * P], colb[1], ce_raw[2], start=False, stop=True)
            mm(bank[2][:, 2 * P:3 * P], colb[2], w_gen[:], start=True, stop=True)
            for j in range(2):
                js = slice(j * P, (j + 1) * P)
                mm(bank[3][:, j:j + 1], me_c1[:, js], col["me_bo"], start=True, stop=False)
                mm(bank[3][:, j:j + 1], me_p1[:, js], col["me_bv"], start=False, stop=False)
                mm(bank[3][:, j:j + 1], me_p2[:, js], col["eq_b"], start=False, stop=True)
            for j in range(2):
                mm(bank[3][:, 2 + j:3 + j], w_f1[:, j * P:(j + 1) * P], col["n1b"], start=True, stop=True)
            for c in range(8):
                mm(bank[3][:, 8 + 4 * c:12 + 4 * c], wqT[:, c, :], nk_zT[:, 4 * c:4 * c + 4], start=True, stop=True)
            for c in range(8):
                last = mm(bank[4][0:H * NULLS, 256:256 + P], nv_pad[:, c, :], w_out[:, c, :], start=(c == 0), stop=(c == 7))
            last.then_inc(pe_made, 1)
            pe.wait_ge(all_set, 1)

            def l_apply(g):
                pe.wait_ge(n_x.steps.sem, n_x.steps.at(g))
                turn(bank[6], lambda t: xn[:, t, :]).then_inc(l_turned.sem, 1)

            def l_back(g):
                pe.wait_ge(l_conv.sem, l_conv.at(g))
                turn(bank[6], lambda t: conv[:, 0, t * P:(t + 1) * P]).then_inc(l_turned.sem, 1)

            def l_norm(g):
                pe.wait_ge(n_l.steps.sem, n_l.steps.at(g))
                turn(bank[6], lambda t: xn[:, t, :]).then_inc(l_turned.sem, 1)

            def l_route(g):
                pe.wait_ge(l_cols.sem, l_cols.at(g, 1))
                for t in range(T):
                    last = mm(bank[7][:, 8 * t:8 * t + 8], xlT[:, t * P:(t + 1) * P], w0_router[:], start=True, stop=True)
                last.then_inc(l_routed.sem, 1)

            def l_coef(g):
                pe.wait_ge(l_coefd.sem, l_coefd.at(g))
                for t in range(T):
                    last = nc.tensor.transpose(bank[7][0:E0, t * P:(t + 1) * P], pick0[:, 0, t, :], ident[:])
                last.then_inc(l_routed.sem, 1)

            def l_chunk(g, j):
                js = slice(j * P, (j + 1) * P)
                if j:
                    pe.wait_ge(l_hid.sem, l_hid.at(g, 3 * j))
                mm(bank[4][:], w0_gate[:, js], xlT[:], start=True, stop=True)
                last = mm(bank[5][:], w0_up[:, js], xlT[:], start=True, stop=True)
                if j < J0:
                    pe.wait_ge(l_cols.sem, l_cols.at(g))
                    last = mm(bank[6][:], sel[:, js], coef0T[:], start=True, stop=True)
                last.then_inc(l_gu.sem, 1)

            def l_down_(g):
                pe.wait_ge(l_hid.sem, l_hid.at(g))
                for t in range(T):
                    for j in range(J0 + 1):
                        last = mm(bank[7][:, t * P:(t + 1) * P], hid0[:, j, t * P:(t + 1) * P], w0_down[:, j, :],
                                  start=(j == 0), stop=(j == J0))
                last.then_inc(l_down.sem, 1)

            def a_apply(g):
                pe.wait_ge(n_a.steps.sem, n_a.steps.at(g))
                turn(bank[0], lambda t: xa[:, t, :]).then_inc(a_turned.sem, 1)

            def a_null(g):
                pe.wait_ge(a_cols.sem, a_cols.at(g))
                for t in range(T):
                    last = mm(bank[3][:, 32 * t:32 * t + 32], xaT[:, t * P:(t + 1) * P], w_nk[:], start=True, stop=True)
                last.then_inc(a_nulls.sem, 1)

            ITEM_BANK = (2, 3, 0, 1)

            def a_proj_(g, t):
                xt = xaT[:, t * P:(t + 1) * P]
                for k in range(4):
                    w = (w_kv, w_kv, w_q, w_q)[k][:, 512 * (k % 2):512 * (k % 2) + 512]
                    if k < 2:
                        if t:
                            pe.wait_ge(a_flat.sem, a_flat.at(g, 4 * (t - 1) + k + 1))
                        elif k == 1:
                            pe.wait_ge(a_nullc.sem, a_nullc.at(g, 1))
                    elif t:
                        pe.wait_ge(a_vals.sem, a_vals.at(g, 2 * (t - 1) + k - 1))
                    mm(bank[ITEM_BANK[k]][:], xt, w, start=True, stop=True).then_inc(a_proj.sem, 1)

            def a_turn_(g, t):
                for k in range(4):
                    pe.wait_ge(a_unit.sem, a_unit.at(g, 4 * t + k + 1))
                    turn(bank[ITEM_BANK[k]], lambda c: unit[:, k, c * P:(c + 1) * P]).then_inc(a_turn.sem, 1)

            def a_value(g, t):
                for k in range(2):
                    pe.wait_ge(a_flat.sem, a_flat.at(g, 4 * t + 3 + k))
                    mm(bank[k][:], xaT[:, t * P:(t + 1) * P], w_kv[:, H * DH + 512 * k:H * DH + 512 * k + 512],
                       start=True, stop=True).then_inc(a_v.sem, 1)

            def a_scores(g, h):
                s, c = h % 2, h // 2
                rs = slice(64 * s, 64 * s + 64)
                if h < 2:
                    pe.wait_ge(a_vals.sem, a_vals.at(g, 2 * T - 1 + h))
                else:
                    pe.wait_ge(a_exp.sem, a_exp.at(g, 2 * (h - 2) + 1))
                for t in range(T):
                    ts = slice(t * P, (t + 1) * P)
                    last = mm(bank[s][:, ts], kT[rs, c, ts], qT[rs, c, ts], start=True, stop=True)
                last.then_inc(a_s.sem, 1)
                if h:
                    pe.wait_ge(a_exp.sem, a_exp.at(g, 2 * h))
                for b in range(SEQ):
                    last = mm(bank[2][:, b * P:(b + 1) * P], kT[rs, c, 2 * b * P:(2 * b + 1) * P],
                              qT[rs, c, (2 * b + 1) * P:(2 * b + 2) * P], start=True, stop=True)
                last.then_inc(a_s.sem, 1)

            def a_mix_(g, h):
                s = h % 2
                pe.wait_ge(a_mask.sem, a_mask.at(g, h + 1))
                pe.wait_ge(a_exp.sem, a_exp.at(g, 2 * h + 2))
                if h:
                    pe.wait_ge(a_mix.sem, a_mix.at(g, 3 * h))
                for t in range(T):
                    dst = bank[3][:, t * (DH + 1):(t + 1) * (DH + 1)]
                    last = mm(dst, p_diag[:, s, t * P:(t + 1) * P], val[:, t, h, :], start=True, stop=(t % 2 == 0))
                    if t % 2:
                        last = mm(dst, p_off[:, s, (t // 2) * P:(t // 2 + 1) * P], val[:, t - 1, h, :], start=False, stop=True)
                last.then_inc(a_pv.sem, 1)

            def a_oT_(g):
                pe.wait_ge(a_pn.sem, a_pn.at(g))
                for t in range(T):
                    last = nc.tensor.transpose(bank[3][0:H * NULLS, t * P:(t + 1) * P],
                                               null_p[:, t, :, :].rearrange("p h n -> p (h n)"), ident[:])
                last.then_inc(a_oT.sem, 1)
                for c in range(8):
                    if c >= 3:
                        pe.wait_ge(a_oc.sem, a_oc.at(g, c - 1))
                    turn(bank[c % 3], lambda t: mixed[:, t, c * P:(c + 1) * P]).then_inc(a_oT.sem, 1)

            def a_out_(g):
                pe.wait_ge(a_oc.sem, a_oc.at(g))
                for t in range(T):
                    ts = slice(t * P, (t + 1) * P)
                    for c in range(8):
                        mm(bank[3][:, ts], outT[:, c, ts], w_out[:, c, :], start=(c == 0), stop=False)
                    last = mm(bank[3][:, ts], null_pT[:, ts], w_nv[:], start=False, stop=True)
                last.then_inc(a_out.sem, 1)

            def f_apply(g):
                pe.wait_ge(n_m.steps.sem, n_m.steps.at(g))
                turn(bank[4], lambda t: x4m[:, t, :]).then_inc(f_turned.sem, 1)

            def f_route(g):
                pe.wait_ge(f_cols.sem, f_cols.at(g))
                for t in range(T):
                    last = mm(bank[7][:, 8 * t:8 * t + 8], xmT[:, t * P:(t + 1) * P], w1_router[:], start=True, stop=True)
                last.then_inc(f_routed.sem, 1)

            def f_ce_(g):
                for t in range(T):
                    last = mm(bank[6][:, t * P:(t + 1) * P], xmT[:, t * P:(t + 1) * P], w_ce[:], start=True, stop=True)
                last.then_inc(f_ce.sem, 1)

            def f_sw(g, j):
                js = slice(j * P, (j + 1) * P)
                if j:
                    pe.wait_ge(f_hid.sem, f_hid.at(g, 2 * j))
                mm(bank[4][:], w_sw1[:, js], xmT[:], start=True, stop=True)
                mm(bank[5][:], w_sw3[:, js], xmT[:], start=True, stop=True).then_inc(f_gu.sem, 1)

            def f_me_(g, j):
                js = slice(j * P, (j + 1) * P)
                if j:
                    pe.wait_ge(f_meg.sem, f_meg.at(g, 1))
                    pe.wait_ge(f_relu.sem, f_relu.at(g, 2))
                else:
                    pe.wait_ge(f_pick.sem, f_pick.at(g, 1))
                mm(bank[7][:], w_me[:, js], xmT[:], start=True, stop=True).then_inc(f_me.sem, 1)

            def f_ml_(g, j):
                js = slice(j * P, (j + 1) * P)
                if j < 2:
                    pe.wait_ge(f_hid.sem, f_hid.at(g))
                else:
                    pe.wait_ge(f_mlg.sem, f_mlg.at(g, j - 1))
                mm(bank[4 + j % 2][:], w_ml1[:, js], xmT[:], start=True, stop=True).then_inc(f_ml.sem, 1)

            def f_ce_apply(g):
                pe.wait_ge(n_c.steps.sem, n_c.steps.at(g))
                turn(bank[6], lambda t: ce_rows[:, t, :]).then_inc(f_ce.sem, 1)

            def f_relu_(g, j):
                js = slice(j * P, (j + 1) * P)
                pe.wait_ge(f_cec.sem, f_cec.at(g, 1))
                if j:
                    pe.wait_ge(f_meg.sem, f_meg.at(g, 1))
                mm(bank[6 + j][:], w_f1[:, js], ce_T, start=True, stop=True).then_inc(f_r.sem, 1)

            def f_ce2(g):
                pe.wait_ge(f_relu.sem, f_relu.at(g))
                for t in range(T):
                    ts = slice(t * P, (t + 1) * P)
                    for j in range(2):
                        last = mm(bank[6][:, ts], hid_relu[j][:, ts], w_f2[:, j, :], start=(j == 0), stop=(j == 1))
                last.then_inc(f_ce.sem, 1)

            def f_ce2_apply(g):
                pe.wait_ge(n_c2.steps.sem, n_c2.steps.at(g))
                turn(bank[6], lambda t: ce_rows[:, t, :]).then_inc(f_gT.sem, 1)

            def f_out(g, t):
                ts = slice(t * P, (t + 1) * P)
                if t == 0:
                    pe.wait_ge(f_mlg.sem, f_mlg.at(g))
                    pe.wait_ge(f_meg.sem, f_meg.at(g))
                    pe.wait_ge(f_cec.sem, f_cec.at(g))
                out_b = bank[4 + t]
                for j in range(J1):
                    mm(out_b[:, 0:P], hid_sw[j][:, ts], w_sw2[:, j, :], start=(j == 0), stop=(j == J1 - 1))
                for j in range(2):
                    mm(out_b[:, P:2 * P], hid_me[j][:, ts], w_c2[:, j, :], start=(j == 0), stop=(j == 1))
                mm(out_b[:, 2 * P:3 * P], ce_T[:, ts], w_gen[:], start=True, stop=True)
                for j in range(J1):
                    last = mm(out_b[:, 3 * P:], hid_ml[j][:, ts], w_ml2[:, j, :], start=(j == 0), stop=(j == J1 - 1))
                last.then_inc(f_e.sem, 1)

            plan(pe, {
                "l_apply": l_apply, "l_back": l_back, "l_norm": l_norm, "l_route": l_route, "l_coef": l_coef,
                "l_chunk": l_chunk, "l_down": l_down_,
                "a_apply": a_apply, "a_null": a_null, "a_proj": a_proj_, "a_turn": a_turn_, "a_value": a_value,
                "a_scores": a_scores, "a_mix": a_mix_, "a_oT": a_oT_, "a_out": a_out_,
                "f_apply": f_apply, "f_route": f_route, "f_ce": f_ce_, "f_sw": f_sw, "f_me": f_me_, "f_ml": f_ml_,
                "f_ce_apply": f_ce_apply, "f_relu": f_relu_, "f_ce2": f_ce2, "f_ce2_apply": f_ce2_apply, "f_out": f_out,
            })


def build(nc, inputs, store_what="x4"):
    arrays, args = {}, {}
    for name, value in inputs.items():
        v = np.ascontiguousarray(value)
        arrays[f"in_{name}"] = v
        args[name] = nc.dram_tensor(f"in_{name}", v.shape, mybir.dt.from_np(v.dtype), kind="ExternalInput").ap()
    out = nc.dram_tensor("out_0", inputs["L0_attn_x"].shape, F32, kind="ExternalOutput").ap()
    program(nc, args, out, store_what)
    return arrays


def kernel(**inputs):
    import concourse.bacc as bacc
    from concourse.bass_utils import run_bass_kernel_spmd

    nc = bacc.Bacc("TRN2", target_bir_lowering=False, num_devices=1)
    arrays = build(nc, inputs)
    r = run_bass_kernel_spmd(nc, [arrays], core_ids=[0])
    return r.results[0]["out_0"]
```

```python
from contextlib import ExitStack

import numpy as np
from concourse import mybir

F32 = mybir.dt.float32
F32R = mybir.dt.float32r
I32 = mybir.dt.int32
U32 = mybir.dt.uint32
ALU = mybir.AluOpType
ACT = mybir.ActivationFunctionType
AX_X = mybir.AxisListType.X

P = 128
EPS = 1e-5
TWO_PI = 6.283185307179586
ROUND = 12582912.0


ORDER = """
f_stats a_ss.0.0 a_m.0 f_apply a_ss.0.1 a_m.1 a_null a_u.0.0 f_turn a_ss.1.0 f_route a_u.0.1 f_ce f_sw.0 f_me.0
f_hid.0 a_ss.1.1 f_ce_apply f_pick a_u.1.0 f_hid.1 a_ss.2.0 a_t.0 a_u.1.1 f_sw.1 f_ceT a_m.2 f_relu.0 f_hid.2
f_sw.2 a_keep a_ss.2.1 a_v.0 f_relu.1 a_u.2.0 f_ce2 a_t.1 l_turn2 a_m.3 a_ss.3.0 a_u.2.1 a_ss.3.1 a_v.1 f_hid.3
f_sw.3 a_t.2 l_res f_ce2_apply a_u.3.0 f_me.1 f_bias l_norm f_ml.0 f_ml.1 a_u.3.1 f_ce2T f_ml.2 l_turn3 a_t.3
l_route l_pick a_v.2 f_ml.3 a_v.3 f_out.0 f_out.1 f_out.2 a_nexp f_out.3 a_scores.0 a_scores.1 f_end_stats
l_coef l_exp l_u.0 a_mix.0 e_stats l_g.0 f_end a_scores.2 l_hg.0 a_mix.1 l_cT a_scores.3 a_mix.2 e_apply
a_scores.4 l_g.1 a_mix.3 l_hg.1 e_turn1 a_scores.5 a_oT.0 l_c.0 e_scan l_g.2 a_mix.4 a_oT.1 l_hu.0 a_scores.6
l_u.1 l_hc.0 a_mix.5 l_c.1 l_hu.1 e_sum a_scores.7 a_mix.6 l_hg.2 a_oT.2 a_scores.8 a_scores.9 a_mix.7 l_hc.1
l_u.2 l_hu.2 l_g.3 a_mix.8 l_hc.2 a_scores.10 a_oT.3 a_mix.9 l_c.2 a_scores.11 l_u.3 a_mix.10 a_scores.12 a_oT.4
l_hg.3 l_hu.3 l_c.3 a_mix.11 a_scores.13 a_mix.12 l_g.4 a_scores.14 l_hg.4 l_hc.3 a_mix.13 a_scores.15 l_hu.4
a_mix.14 a_oT.5 l_u.4 l_down.0 a_mix.15 l_down.1 a_oT.6 a_oT.7 a_oT.8 l_dstats l_end l_down.2 l_astats l_down.3
l_aapply a_o a_out l_x l_xl a_end
"""


PROLOGUE = """
e_stats s_phase e_apply s_conv e_turn1 e_scan s_w0 e_sum l_turn2 s_alibi l_res s_scale s_raw s_turn l_norm
l_turn3 l_route l_pick l_exp l_coef l_cT s_fold1 l_g.0 s_pad s_fold2 l_hg.0 s_v2 l_u.0 s_fold3 l_c.0 s_fold4
l_hu.0 l_g.1 l_g.2 l_hc.0 l_hg.1 s_bias l_u.1 l_c.1 l_hu.1 l_hc.1 E_stats l_c.2 l_hg.2 l_u.2 l_hu.2 l_hg.3 l_g.3
l_u.3 E_apply l_hc.2 s_split l_c.3 l_hu.3 l_g.4 l_hc.3 l_hg.4 l_u.4 l_hu.4 E_turn1 E_scan l_down.0 l_down.1
l_down.2 l_down.3 l_dstats l_end l_astats E_sum l_aapply l_xl l_x
"""


class Signal:

    def __init__(self, sem, per):
        self.sem, self.per = sem, per

    def at(self, g, n=None):
        return g * self.per + (self.per if n is None else n)


class Norm:

    def __init__(self, sb, signal, name, more=0, twice=False):
        self.six = sb(name + "_six", [P, 4, 6])
        self.mv = sb(name + "_mv", [P, 4, 2])
        self.var = sb(name + "_var", [P, 4])
        self.rstd = sb(name + "_rstd", [P, 4])
        self.steps = signal(name + "_steps", 13 + more)
        self.rooted = signal(name + "_rooted", 1)
        self.scale, self.add = (1.0 + EPS, EPS * EPS) if twice else (1.0, EPS)


def program(nc, a, out):
    x = a["L0_attn_x"]
    B, L, D = x.shape
    SEQ = 2
    G = B // SEQ
    T = SEQ * L // P
    N = T * P
    H, DH, NULLS = 16, 64, 2
    E0 = a["L0_ffn_router"].shape[1]
    HID0 = a["L0_ffn_experts_gate"].shape[2] * E0
    J0 = HID0 // P
    I1 = a["L1_ffn_sw_w1"].shape[1]
    J1 = I1 // P
    E1 = a["L1_ffn_router_w"].shape[1]
    assert D == P and L == 2 * P and T == 4 and N == 512 and E0 == 8 and G >= 4

    start = 2.0 ** (-2.0 ** (-1.0))
    SLOPES = [start * start ** i for i in range(H)]
    MID = P // 2 - 1
    LOW = 32

    with ExitStack() as ctx:
        def sb(name, shape, dt=F32):
            return ctx.enter_context(nc.sbuf_tensor(name, shape, dt))

        def sem(name):
            return ctx.enter_context(nc.semaphore(name))

        def signal(name, per):
            return Signal(sem(name), per)

        bank = [ctx.enter_context(nc.psum_tensor(f"bank{i}", [P, 512], F32)) for i in range(8)]

        class Split:
            def __init__(self, hi, lo):
                self.hi, self.lo = hi, lo

            def __getitem__(self, at):
                return Split(self.hi[at], self.lo[at])

        def split_weight(name, width):
            return Split(sb(name + "_hi", [P, width], F32R)[:], sb(name + "_lo", [P, width], F32R)[:])

        ident = sb("ident", [P, P])
        causal = sb("causal", [P, P])
        expert_no = sb("expert_no", [P, 4, 8])
        minus_half = sb("minus_half", [P, 16])
        sel = sb("sel", [LOW + E0, HID0], F32R)
        part_no = sb("part_no", [P, 1])
        cos_t = sb("cos_t", [P, L + 1])
        sin_t = sb("sin_t", [P, L + 1])
        conv_a = sb("conv_a", [P, L])
        conv_b = sb("conv_b", [P, L])
        conv_c = sb("conv_c", [P, L])
        decay_row = sb("decay_row", [P, N])
        vec = sb("vec", [P, 40])
        slope = sb("slope", [P, H])
        bias_diag = sb("bias_diag", [P, H])
        bias_off = sb("bias_off", [P, H])
        bias_null = sb("bias_null", [P, T, H, NULLS])
        qk_scale = sb("qk_scale", [P, 1])
        w0_router = split_weight("w0_router", E0)
        w0_gate = split_weight("w0_gate", HID0 + P)
        w0_up = split_weight("w0_up", HID0 + P)
        w0_down = sb("w0_down", [P, J0 + 1, P])
        w_q = split_weight("w_q", H * DH)
        w_kv = split_weight("w_kv", 2 * H * DH)
        w_out = sb("w_out", [P, H * DH // P, P])
        w_nk = split_weight("w_nk", H * NULLS)
        w_nv = sb("w_nv", [H * NULLS, P])
        w1_router = sb("w1_router", [P, 8])
        b1_router = sb("b1_router", [P, 8])
        w_sw1 = sb("w_sw1", [P, I1])
        w_sw3 = sb("w_sw3", [P, I1])
        w_sw2 = sb("w_sw2", [P, J1, P])
        w_me = sb("w_me", [P, 2 * P])
        w_c2 = sb("w_c2", [P, 2, P])
        w_ce = sb("w_ce", [P, P])
        w_f1 = sb("w_f1", [P, 2 * P])
        w_f2 = sb("w_f2", [P, 2, P])
        w_gen = sb("w_gen", [P, P])
        w_ml1 = sb("w_ml1", [P, I1])
        w_ml2 = sb("w_ml2", [P, J1, P])
        b_me = sb("b_me", [P, 2])
        b_f1 = sb("b_f1", [P, 2])
        b_ml = sb("b_ml", [P, J1])
        row_ce = sb("row_ce", [P, P])
        row_g1 = sb("row_g1", [P, P])
        row_res = sb("row_res", [P, P])
        row_out = sb("row_out", [P, E1, P])

        xin = sb("xin", [P, T, D])
        xn = sb("xn", [P, T, D])
        x1 = sb("x1", [P, T, D])
        x2n = sb("x2n", [P, T, D])
        x2 = sb("x2", [P, T, D])
        x3 = sb("x3", [P, T, D])
        x4 = sb("x4", [P, T, D])
        x4m = sb("x4m", [P, T, D])
        xlT = split_weight("xlT", N)
        xaT = split_weight("xaT", N)
        xmT = sb("xmT", [P, N])
        conv = sb("conv", [P, 4, N])
        tanh1 = sb("tanh1", [P, N])
        tanh0 = sb("tanh0", [P, N])[:]
        ce_rows = sb("ce_rows", [P, T, D])
        ce_T = x4m[:].rearrange("p t d -> p (t d)")
        xa = ce_rows
        logit0 = sb("logit0", [P, T, 8])
        top0 = sb("top0", [P, T, 8])
        idx0 = sb("idx0", [P, T, 8], U32)
        idf0 = sb("idf0", [P, T, 2])
        exp0 = sb("exp0", [P, T, 8])
        sum0 = sb("sum0", [P, T])
        prob0 = sb("prob0", [P, T, 2])
        pick0 = sb("pick0", [P, 2, T, 8])
        coef0 = sb("coef0", [LOW + E0, N], F32R)
        coef0T = Split(coef0[0:E0, :], coef0[LOW:LOW + E0, :])
        square = sb("square", [P, 4, 512])
        sumsq = sb("sumsq", [P, 2, 2, 16])
        rnorm = sb("rnorm", [P, 2, T, 16])
        unit = sb("unit", [P, 2, 4, 512])
        qT = sb("qT", [P, 8, N])
        kT = sb("kT", [P, 8, N])
        val = sb("val", [P, T, H, DH + 1])
        null_s = sb("null_s", [P, T, H, NULLS])
        null_p = sb("null_p", [P, T, H, NULLS])
        null_sum = sb("null_sum", [P, T, H])
        denom = sb("denom", [P, T])
        recip = sb("recip", [P, T, H])
        mixed = sb("mixed", [P, T, H * DH])
        logit1 = sb("logit1", [P, T, 8])
        top1 = sb("top1", [P, T, 8])
        idx1 = sb("idx1", [P, T, 8], U32)
        idf1 = sb("idf1", [P, T, 2])
        gap1 = sb("gap1", [P, T])
        wt1 = sb("wt1", [P, T, 2])
        pick1 = sb("pick1", [P, 2, T, 8])
        unit_flat = unit[:].rearrange("p a k c -> p (a k c)")
        hid0 = unit_flat[:, 0:(J0 + 1) * N].rearrange("p (j n) -> p j n", n=N)
        p_diag = unit_flat[:, 5 * N:7 * N].rearrange("p (k n) -> p k n", n=N)
        p_off = unit_flat[:, 7 * N:8 * N].rearrange("p (k n) -> p k n", k=2)
        mixed_flat = mixed[:].rearrange("p t c -> p (t c)").rearrange("p (j n) -> p j n", n=N)
        hid_sw = [mixed_flat[:, j, :] for j in range(4)]
        hid_me = [mixed_flat[:, 4 + j, :] for j in range(2)]
        hid_relu = [mixed_flat[:, 6 + j, :] for j in range(2)]
        hid_ml = [square[:, j, :] for j in range(4)]
        null_pT = tanh1[0:H * NULLS, :]
        mix_bias = ce_rows[:]
        ce_res = x4[:]
        outT = qT

        vlist = ["angle", "lnabs", "scale", "init_re", "init_im", "last_re", "last_im", "decay", "z",
                 "nz", "theta", "r", "gate", "gamma", "qs", "ks", "eq_b", "me_bv", "me_bo", "syn_b",
                 "ce_bv", "n1b", "n2b", "n1g", "n2g"]
        col = {n: vec[:, i:i + 1] for i, n in enumerate(vlist)}
        c1b = vec[:, 26:28]
        f1b = vec[:, 28:30]

        nk_rows = mixed[0:32, 0, 0:64]
        nv_rows = mixed[0:32, 0, 64:128]
        qs_row = mixed[0:32, 0, 128:192]
        ks_row = mixed[0:32, 0, 192:256]
        nk_sq = mixed[0:32, 0, 256:320]
        nk_z = mixed[0:32, 0, 320:448]
        nv_z = mixed[0:32, 0, 448:576]
        par_i = sb("par_i", [32, 2], I32)
        par = mixed[0:32, 0, 576:578]
        nk_ss = mixed[0:32, 0, 578:580]
        nk_zT = mixed[:, 0, 640:672]
        nv_zT = mixed[:, 0, 672:704]
        nv_pad = mixed[:, 1, 0:256].rearrange("p (c r) -> p c r", c=8)
        me_raw = [mixed[:, 2, 128 * i:128 * i + 128] for i in range(3)]
        me_c1 = mixed[:, 2, 384:640]
        me_p1 = mixed[:, 2, 640:896]
        me_p2 = mixed[:, 3, 0:256]
        ce_raw = [mixed[:, 3, 256 + 128 * i:384 + 128 * i] for i in range(3)]
        ce_v2 = mixed[:, 3, 640:768]
        time = kT[:, 0, 0:L + 1]
        phase = kT[:, 1, 0:L + 1]
        turns = kT[:, 2, 0:L + 1]
        frac = kT[:, 3, 0:L + 1]
        rpow = kT[:, 4, 0:L + 1]
        part_a = kT[:, 5, 0:L + 1]
        part_b = kT[:, 6, 0:L + 1]
        wT = [kT[:, 7, 128 * i:128 * i + 128] for i in range(4)] + [qT[:, 7, 128 * i:128 * i + 128] for i in range(3)]
        wqT = qT[:, 0:2, :].rearrange("p a (c n) -> p (a c) n", n=P)
        colb = [qT[:, 2, 128 * i:128 * i + 128] for i in range(3)]
        row_tmp = [qT[:, 3, 128 * i:128 * i + 128] for i in range(4)]
        lb_row = qT[:, 4, 0:8]
        w0_gate_raw = unit_flat[:, 0:HID0 + P]
        w0_up_raw = unit_flat[:, HID0 + P:2 * (HID0 + P)]
        w0_router_raw = unit_flat[:, 2 * (HID0 + P):2 * (HID0 + P) + E0]
        w_q_raw = unit_flat[:, 5 * N:5 * N + H * DH]
        w_kv_raw = square[:].rearrange("p k n -> p (k n)")
        sel_f = qT[0:LOW + E0, 5, :]
        zraw = sb("zraw", [P, 2])

        loaded0 = sem("loaded0")
        loaded1 = sem("loaded1")
        loaded2 = sem("loaded2")
        loaded3 = sem("loaded3")
        made = sem("made")
        pool_made = sem("pool_made")
        act_made = sem("act_made")
        pe_made = sem("pe_made")
        z_made = sem("z_made")
        phase_made = sem("phase_made")
        w0_made = sem("w0_made")
        nk_summed = sem("nk_summed")
        raw_made = sem("raw_made")
        pad_made = sem("pad_made")
        v2_made = sem("v2_made")
        all_set = sem("all_set")
        dve_passed = sem("dve_passed")
        pool_passed = sem("pool_passed")

        x_loaded = signal("x_loaded", 16)
        stored = signal("stored", 16)
        n_x = Norm(sb, signal, "n_x")
        n_y = Norm(sb, signal, "n_y", more=1)
        n_l = Norm(sb, signal, "n_l")
        n_d = Norm(sb, signal, "n_d", more=1)
        n_a = Norm(sb, signal, "n_a", twice=True)
        n_o = Norm(sb, signal, "n_o", more=1)
        n_m = Norm(sb, signal, "n_m")
        n_c = Norm(sb, signal, "n_c")
        n_c2 = Norm(sb, signal, "n_c2")
        n_f = Norm(sb, signal, "n_f", more=1)
        def table(text):
            return [(n, *map(int, rest)) for n, *rest in (step.split(".") for step in text.split())]

        def order(e, l, m, f):
            return [s for s in table(ORDER) if {"e": e, "l": l, "a": m, "f": f}[s[0][0]]]

        ring = [(s[0][2], *s[1:], k) for s in order(1, 1, 1, 1) if s[0] in ("a_m", "a_t", "a_v")
                for k in range(2 if s[0] == "a_v" else 4)]
        USES = len(ring)

        def use(kind, t=0, k=0):
            return ring.index((kind, t, k))


        l_turned = signal("l_turned", 3)
        l_conv = signal("l_conv", 6)
        l_gain = signal("l_gain", 2)
        l_cols = signal("l_cols", 2)
        l_routed = signal("l_routed", 2)
        l_pick = signal("l_pick", 10 + 2 * T)
        l_coefd = signal("l_coefd", 1)
        l_exp = signal("l_exp", 1)
        l_g = signal("l_g", J0 + 1)
        l_u = signal("l_u", J0 + 1)
        l_c = signal("l_c", J0)
        l_tanh = signal("l_tanh", J0 + 1)
        l_hg = signal("l_hg", J0 + 1)
        l_hu = signal("l_hu", J0 + 1)
        l_hc = signal("l_hc", J0)
        l_down = signal("l_down", T)
        a_kept = signal("a_kept", 1)
        l_low = signal("l_low", 3)
        l_xt = signal("l_xt", 1)
        l_xc = signal("l_xc", 1)
        a_put = signal("a_put", USES)
        a_took = signal("a_took", USES)
        a_nulls = signal("a_nulls", 1)
        a_nullc = signal("a_nullc", 4)
        a_nexp = signal("a_nexp", 1)
        a_sq = signal("a_sq", 4 * T)
        a_ss = signal("a_ss", 4 * T)
        a_root = signal("a_root", 2 * T)
        a_unit = signal("a_unit", 2 * T)
        a_s = signal("a_s", 2 * H)
        a_exp = signal("a_exp", 2 * H)
        a_mask = signal("a_mask", H)
        a_pv = signal("a_pv", H)
        a_mix = signal("a_mix", 3 * H)
        a_pn = signal("a_pn", 1)
        a_oT = signal("a_ot", 9)
        a_oc = signal("a_oc", 9)
        a_out = signal("a_out", 1)
        f_turned = signal("f_turned", 1)
        f_cols = signal("f_cols", 1)
        f_routed = signal("f_routed", 1)
        f_pick = signal("f_pick", 9 + 2 * T)
        f_coefd = signal("f_coefd", 1)
        f_gap = signal("f_gap", 1)
        f_gu = signal("f_gu", J1)
        f_tanh = signal("f_tanh", J1)
        f_hid = signal("f_hid", 2 * J1)
        f_me = signal("f_me", 2)
        f_meg = signal("f_meg", 2)
        f_ml = signal("f_ml", J1)
        f_mlg = signal("f_mlg", J1)
        f_ce = signal("f_ce", 3)
        f_ced = signal("f_ced", 2)
        f_res = signal("f_res", 2)
        f_cec = signal("f_cec", 2)
        f_r = signal("f_r", 2)
        f_relu = signal("f_relu", 2)
        f_gT = signal("f_gT", 1)
        f_e = signal("f_e", T)
        f_bias = signal("f_bias", 5)
        f_eb = signal("f_eb", E1 * T)

        def rows3(ap):
            return ap.rearrange("p (t d) -> p t d", t=T)

        LOADS2, LOADS3 = 25, 25
        POOL_MADE = 10 + H + 5 + 6
        ACT_MADE = 17

        block = ctx.enter_context(nc.Block())

        def play(steps, S, **group):
            for name, *rest in S:
                if name.lower() in steps:
                    steps[name.lower()](*([] if name[0] == "s" else [group[name[0]]]), *rest)

        def plan(eng, steps):
            play(steps, table(PROLOGUE), e=0, l=0, E=1)
            play(steps, order(1, 1, 1, 0), e=2, l=1, a=0)
            with eng.Fori(1, G - 2) as i:
                play(steps, order(1, 1, 1, 1), e=i + 2, l=i + 1, a=i, f=i - 1)
            play(steps, order(0, 1, 1, 1), l=G - 1, a=G - 2, f=G - 3)
            play(steps, order(0, 0, 1, 1), a=G - 1, f=G - 2)
            play(steps, order(0, 0, 0, 1), f=G - 1)

        def known(g):
            return isinstance(g, int)

        def first(g):
            return known(g) and g == 0

        xv = x.rearrange("(g s) (b p) d -> g p (s b) d", s=SEQ, p=P)
        ov = out.rearrange("(g s) (b p) d -> g p (s b) d", s=SEQ, p=P)

        column = lambda v: v.rearrange("(p a) -> p a", a=1)
        columns = lambda v: v.rearrange("(c p) -> p c", p=P)
        row = lambda v, n=P: v.partition_broadcast(n)
        nkv = a["L1_attn_null_kv"].rearrange("h (n two) d -> (h n) two d", two=2)
        loads = [
            (w_q_raw, a["L1_attn_w_q"]), (w_kv_raw, a["L1_attn_w_kv"]),
            (w_out[:], a["L1_attn_w_out"].rearrange("(c p) d -> p c d", p=P)),
            (col["gamma"], column(a["L1_attn_gamma"])),
            (vec[0:64, 14:15], column(a["L1_attn_q_scale"])), (vec[64:128, 14:15], column(a["L1_attn_q_scale"])),
            (vec[0:64, 15:16], column(a["L1_attn_k_scale"])), (vec[64:128, 15:16], column(a["L1_attn_k_scale"])),
            (qs_row, row(a["L1_attn_q_scale"], 32)), (ks_row, row(a["L1_attn_k_scale"], 32)),
            (nk_rows, nkv[:, 0, :]), (nv_rows, nkv[:, 1, :]),
            (w1_router[:, 0:E1], a["L1_ffn_router_w"]),
            (b1_router[:, 0:E1], row(a["L1_ffn_router_b"])), (lb_row[:, 0:E1], row(a["L1_ffn_load_balancer"])),
            (w_sw1[:], a["L1_ffn_sw_w1"]), (w_sw3[:], a["L1_ffn_sw_w3"]),
            (w_sw2[:], a["L1_ffn_sw_w2"].rearrange("(c p) d -> p c d", p=P)),
            (me_raw[0], a["L1_ffn_me_eq_w"]), (me_raw[1], a["L1_ffn_me_wv"]), (me_raw[2], a["L1_ffn_me_wo"]),
            (me_c1, a["L1_ffn_me_c1w"]), (w_c2[:], a["L1_ffn_me_c2w"].rearrange("(c p) d -> p c d", p=P)),
            (col["eq_b"], column(a["L1_ffn_me_eq_b"])), (col["me_bv"], column(a["L1_ffn_me_bv"])),
            (col["me_bo"], column(a["L1_ffn_me_bo"])), (c1b, columns(a["L1_ffn_me_c1b"])),
            (ce_raw[0], a["L1_ffn_ce_syn_w"]), (ce_raw[1], a["L1_ffn_ce_wv"]), (ce_raw[2], a["L1_ffn_ce_wo"]),
            (col["syn_b"], column(a["L1_ffn_ce_syn_b"])), (col["ce_bv"], column(a["L1_ffn_ce_bv"])),
            (row_tmp[0], row(a["L1_ffn_ce_bo"])), (row_tmp[1], row(a["L1_ffn_ce_f2b"])),
            (row_tmp[2], row(a["L1_ffn_ce_gen_b"])), (row_tmp[3], row(a["L1_ffn_ce_n1b"])),
            (row_g1[:], row(a["L1_ffn_ce_n1g"])),
            (col["n1g"], column(a["L1_ffn_ce_n1g"])), (col["n1b"], column(a["L1_ffn_ce_n1b"])),
            (col["n2g"], column(a["L1_ffn_ce_n2g"])), (col["n2b"], column(a["L1_ffn_ce_n2b"])),
            (w_f1[:], a["L1_ffn_ce_f1w"]), (w_f2[:], a["L1_ffn_ce_f2w"].rearrange("(c p) d -> p c d", p=P)),
            (f1b, columns(a["L1_ffn_ce_f1b"])), (w_gen[:], a["L1_ffn_ce_gen_w"]),
            (w_ml1[:], a["L1_ffn_ml_w1"]), (w_ml2[:], a["L1_ffn_ml_w2"].rearrange("(c p) d -> p c d", p=P)),
            (b_ml[:], columns(a["L1_ffn_ml_b1"])),
            (row_out[:, 1, :], row(a["L1_ffn_me_c2b"])), (row_out[:, 3, :], row(a["L1_ffn_ml_b2"])),
        ]
        assert len(loads) == LOADS2 + LOADS3

        @block.sync
        def _(sp):
            def load_x(g):
                if not first(g):
                    sp.wait_ge(n_y.steps.sem, n_y.steps.at(g - 1))
                sp.dma_start(xin[:], xv[g]).then_inc(x_loaded.sem, 16)

            def store(g):
                sp.wait_ge(n_f.steps.sem, n_f.steps.at(g))
                sp.dma_start(ov[g], x4[:]).then_inc(stored.sem, 16)

            sp.sem_inc(stored.sem, stored.per)
            load_x(0)
            for name, v in (("lnabs", "L0_attn_ln_minus_ln_phazor_abs"), ("angle", "L0_attn_phazor_angle"),
                            ("scale", "L0_attn_ln_phazor_scale"), ("init_re", "L0_attn_phazor_init_re"),
                            ("init_im", "L0_attn_phazor_init_im"), ("last_re", "L0_attn_last_conv_re"),
                            ("last_im", "L0_attn_last_conv_im")):
                sp.dma_start(col[name], column(a[v])).then_inc(loaded0, 16)
            for dst, src in (
                (w0_router_raw, a["L0_ffn_router"]),
                (w0_gate_raw[:, 0:HID0].rearrange("p (e d) -> p e d", e=E0), a["L0_ffn_experts_gate"].rearrange("e h d -> h e d")),
                (w0_up_raw[:, 0:HID0].rearrange("p (e d) -> p e d", e=E0), a["L0_ffn_experts_up"].rearrange("e h d -> h e d")),
                (w0_gate_raw[:, HID0:], a["L0_ffn_shared_gate"]),
                (w0_up_raw[:, HID0:], a["L0_ffn_shared_up"]),
                (w0_down[:, 0:J0, :], a["L0_ffn_experts_down"].rearrange("e d h -> (e d) h").rearrange("(j p) h -> p j h", p=P)),
                (w0_down[:, J0, :], a["L0_ffn_shared_down"]),
            ):
                sp.dma_start(dst, src).then_inc(loaded1, 16)
            for dst, src in loads[0::2]:
                sp.dma_start(dst, src, allow_slow_non_contiguous=True).then_inc(loaded2, 16)
            load_x(1)
            load_x(2)
            with sp.Fori(1, G - 2) as i:
                load_x(i + 2)
                store(i - 1)
            store(G - 3)
            store(G - 2)
            store(G - 1)
            sp.wait_ge(stored.sem, stored.at(G))

        @block.gpsimd
        def _(pool):
            n = [0]

            def made_by(i):
                n[0] += 1
                i.then_inc(pool_made, 1)

            made_by(pool.memset(ident[:], 0.0))
            made_by(pool.memset(causal[:], 1.0))
            made_by(pool.memset(sel_f, 0.0))
            pool.wait_ge(pool_made, n[0])
            for r in range(2):
                made_by(pool.memset(sel_f[LOW * r:LOW * r + E0, :], 1.0))
                pool.wait_ge(pool_made, n[0])
            made_by(pool.iota(time, pattern=[[1, L + 1]], base=0, channel_multiplier=0, allow_small_or_imprecise_dtypes=True))
            made_by(pool.iota(expert_no[:].rearrange("p t e -> p (t e)"), pattern=[[0, T], [1, 8]], base=0, channel_multiplier=0, allow_small_or_imprecise_dtypes=True))
            made_by(pool.iota(part_no[:], pattern=[[0, 1]], base=0, channel_multiplier=1, allow_small_or_imprecise_dtypes=True))
            made_by(pool.iota(par_i[:], pattern=[[0, 2]], base=0, channel_multiplier=1))
            made_by(pool.memset(minus_half[:], -0.5))
            for h in range(H):
                made_by(pool.memset(slope[:, h:h + 1], SLOPES[h]))
            made_by(pool.memset(val[:, :, :, DH], 1.0))
            made_by(pool.memset(nv_pad, 0.0))
            made_by(pool.memset(w1_router[:, E1:8], 0.0))
            made_by(pool.memset(b1_router[:, E1:8], -1e30))
            made_by(pool.memset(row_out[:, 0, :], 0.0))
            pool.wait_ge(pool_made, n[0])
            made_by(pool.affine_select(out=ident[:], in_=ident[:], compare_op=ALU.not_equal, fill=1.0, base=0,
                                       pattern=[[-1, P]], channel_multiplier=1))
            made_by(pool.affine_select(out=causal[:], in_=causal[:], compare_op=ALU.is_ge, fill=0.0, base=0,
                                       pattern=[[1, P]], channel_multiplier=-1))
            for r in range(2):
                sel_r = sel_f[LOW * r:LOW * r + E0, :]
                made_by(pool.affine_select(out=sel_r, in_=sel_r, compare_op=ALU.is_ge, fill=0.0, base=0,
                                           pattern=[[1, HID0]], channel_multiplier=-(HID0 // E0)))
                pool.wait_ge(pool_made, n[0])
            pool.wait_ge(pool_made, n[0])
            for r in range(2):
                sel_r = sel_f[LOW * r:LOW * r + E0, :]
                made_by(pool.affine_select(out=sel_r, in_=sel_r, compare_op=ALU.is_ge, fill=0.0, base=HID0 // E0 - 1,
                                           pattern=[[-1, HID0]], channel_multiplier=HID0 // E0))
                pool.wait_ge(pool_made, n[0])
            assert n[0] == POOL_MADE

            def null_norms():
                pool.wait_ge(nk_summed, 1)
                pool.tensor_tensor(nk_ss[:, 1:2], nk_ss[:, 0:1], minus_half[0:32, 0:1], ALU.pow).then_inc(pool_made, 1)

            def root(norm):
                def step(g):
                    pool.wait_ge(norm.steps.sem, norm.steps.at(g, 9))
                    pool.tensor_tensor(norm.rstd[:], norm.var[:], minus_half[:, 0:4], ALU.pow).then_inc(norm.rooted.sem, 1)
                return step

            def conv_gains(g):
                for k, w in enumerate((conv_a, conv_b)):
                    pool.wait_ge(l_conv.sem, l_conv.at(g, 3 + k))
                    pool.tensor_tensor(conv[:, k, :].rearrange("p (s t) -> p s t", s=SEQ),
                                       conv[:, 2 + k, :].rearrange("p (s t) -> p s t", s=SEQ),
                                       w[:].unsqueeze(1).to_broadcast([P, SEQ, L]), ALU.mult).then_inc(l_gain.sem, 1)

            def keep_x2(g):
                if not first(g):
                    pool.wait_ge(n_o.steps.sem, n_o.steps.at(g - 1))
                pool.wait_ge(n_d.steps.sem, n_d.steps.at(g))
                pool.sem_inc(pool_passed, 1)
                pool.tensor_copy(x2[:], x2n[:]).then_inc(a_kept.sem, 1)

            def norms(g, t, k):
                pool.wait_ge(a_ss.sem, a_ss.at(g, 4 * t + 2 * (k + 1)))
                pool.tensor_tensor(rnorm[:, k, t, :], sumsq[:, t % 2, k, :], minus_half[:], ALU.pow).then_inc(a_root.sem, 1)

            def mask(g, h):
                pool.wait_ge(a_exp.sem, a_exp.at(g, 2 * h + 1))
                pd = rows3(p_diag[:, h % 2, :])
                pool.tensor_tensor(pd, pd, causal[:].unsqueeze(1).to_broadcast([P, T, P]), ALU.mult).then_inc(a_mask.sem, 1)

            def ce_residual2(g):
                pool.wait_ge(stored.sem, stored.at(g))
                pool.wait_ge(n_c.steps.sem, n_c.steps.at(g))
                pool.tensor_tensor(ce_res, ce_rows[:], row_g1[:].unsqueeze(1).to_broadcast([P, T, D]), ALU.mult).then_inc(f_res.sem, 1)
                pool.wait_ge(f_res.sem, f_res.at(g, 1))
                pool.tensor_tensor(ce_res, ce_res, row_res[:].unsqueeze(1).to_broadcast([P, T, D]), ALU.add).then_inc(f_res.sem, 1)

            def weigh_biases(g):
                pool.wait_ge(f_coefd.sem, f_coefd.at(g))
                pool.wait_ge(f_gT.sem, f_gT.at(g))
                terms = (ce_rows[:], ce_res, ce_res)
                for e in range(1, E1):
                    if e == E1 - 1:
                        pool.wait_ge(f_bias.sem, f_bias.at(g, e))
                    pool.tensor_tensor(terms[e - 1], row_out[:, e, :].unsqueeze(1).to_broadcast([P, T, D]),
                                       pick1[:, 0, :, e:e + 1].to_broadcast([P, T, D]), ALU.mult).then_inc(f_bias.sem, 1)
                    if e > 1:
                        pool.wait_ge(f_bias.sem, f_bias.at(g, 2 * e - 2))
                        pool.tensor_tensor(mix_bias, mix_bias, terms[e - 1], ALU.add).then_inc(f_bias.sem, 1)

            plan(pool, {
                "s_scale": null_norms,
                "e_stats": root(n_x), "e_scan": conv_gains, "l_turn2": root(n_y), "l_res": root(n_l), "l_dstats": root(n_d),
                "l_astats": root(n_a), "a_keep": keep_x2, "a_ss": norms, "a_scores": mask, "a_o": root(n_o),
                "f_stats": root(n_m), "f_ce": root(n_c), "f_ce_apply": ce_residual2, "f_ce2": root(n_c2),
                "f_bias": weigh_biases, "f_end_stats": root(n_f),
            })

        @block.scalar
        def _(act):
            n = [0]

            def made_by(i):
                n[0] += 1
                i.then_inc(act_made, 1)

            act.wait_ge(loaded0, 16 * 7)
            made_by(act.activation(col["decay"], col["lnabs"], ACT.Exp))
            act.wait_ge(z_made, 1)
            made_by(act.activation(col["r"], col["nz"], ACT.Exp))
            act.wait_ge(pool_made, POOL_MADE)
            made_by(act.activation(rpow, time, ACT.Exp, scale=col["nz"]))
            assert n[0] == 3
            act.wait_ge(phase_made, 1)
            made_by(act.activation(sin_t[:], part_a, ACT.Sin, scale=TWO_PI))
            made_by(act.activation(cos_t[:], part_b, ACT.Sin, scale=TWO_PI))
            for dst, src in loads[1::2]:
                act.dma_start(dst, src, allow_slow_non_contiguous=True).then_inc(loaded3, 16)

            def s_turn():
                act.wait_ge(pe_made, 1)
                made_by(act.activation(nk_zT, bank[0][:, 0:32], ACT.Copy))
                made_by(act.activation(nv_zT, bank[0][:, 32:64], ACT.Copy))
                for i in range(2):
                    made_by(act.activation(wT[4 + i], bank[0][:, 128 * (i + 1):128 * (i + 2)], ACT.Copy))
                for k in range(2):
                    act.wait_ge(pe_made, k + 2)
                    made_by(act.activation(wqT[:, 4 * k:4 * k + 4, :], bank[1 + k][:].rearrange("p (c n) -> p c n", n=P), ACT.Copy))
                act.wait_ge(pe_made, 4)
                for i in range(3):
                    made_by(act.activation(wT[i], bank[7][:, 128 * i:128 * i + 128], ACT.Copy))

            def s_fold1():
                act.wait_ge(pe_made, 6)
                made_by(act.activation(me_p1, bank[1][:, 0:256], ACT.Copy))

            def s_fold2():
                act.wait_ge(pe_made, 7)
                made_by(act.activation(me_p2, bank[1][:, 256:512], ACT.Copy))

            def s_fold3():
                act.wait_ge(pe_made, 8)
                made_by(act.activation(w_me[:], bank[2][:, 0:256], ACT.Copy))
                assert n[0] == ACT_MADE

            def to_cols(g):
                act.wait_ge(l_turned.sem, l_turned.at(g, 3))
                act.activation(xlT.hi, bank[3][:], ACT.Copy).then_inc(l_cols.sem, 1)

            def exps0(g):
                act.wait_ge(l_pick.sem, l_pick.at(g, 2 + 2 * T))
                act.activation(exp0[:], exp0[:], ACT.Exp).then_inc(l_exp.sem, 1)

            def coef_cols(g):
                act.wait_ge(l_routed.sem, l_routed.at(g, 2))
                act.activation(coef0T.hi, bank[6][0:E0, :], ACT.Copy).then_inc(l_cols.sem, 1)

            def tanh_l(g, j):
                act.wait_ge(l_g.sem, l_g.at(g, j + 1))
                if j:
                    act.wait_ge(l_hg.sem, l_hg.at(g, j))
                act.activation(tanh0, bank[4][:], ACT.Tanh, scale=0.5).then_inc(l_tanh.sem, 1)

            def xa_cols(g):
                act.wait_ge(l_xt.sem, l_xt.at(g))
                act.activation(xaT.hi, bank[5][:], ACT.Copy).then_inc(l_xc.sem, 1)

            def projected(g, t):
                ahead = 4 if t == 1 else 2
                for k in range(4):
                    if k % ahead == 0:
                        for i in range(k, k + ahead):
                            n = use("m", t, i)
                            act.wait_ge(a_put.sem, a_put.at(g, n + 1))
                            act.activation(unit[:, t % 2, i, :], bank[n % 3][:], ACT.Copy).then_inc(a_took.sem, 1)
                    act.wait_ge(a_took.sem, a_took.at(g, use("m", t, k) + 1))
                    if t:
                        act.wait_ge(a_ss.sem, a_ss.at(g, 4 * (t - 1) + 2 * (k // 2) + 1))
                    elif not first(g):
                        act.wait_ge(a_ss.sem, a_ss.at(g - 1, 4 * (T - 1) + 2 * (k // 2) + 1))
                    act.activation(square[:, k, :], unit[:, t % 2, k, :], ACT.Square).then_inc(a_sq.sem, 1)

            def flat(g, t):
                for k in range(4):
                    n = use("t", t, k)
                    act.wait_ge(a_put.sem, a_put.at(g, n + 1))
                    dst = (kT, kT, qT, qT)[k][:, 4 * (k % 2):4 * (k % 2) + 4, t * P:(t + 1) * P]
                    src = bank[n % 3][:].rearrange("p (c n) -> p c n", n=P)
                    if k < 2:
                        act.activation(dst, src, ACT.Copy).then_inc(a_took.sem, 1)
                    else:
                        act.activation(dst, src, ACT.Copy, scale=qk_scale[:]).then_inc(a_took.sem, 1)

            def values(g, t):
                for k in range(2):
                    n = use("v", t, k)
                    act.wait_ge(a_put.sem, a_put.at(g, n + 1))
                    act.activation(val[:, t, 8 * k:8 * k + 8, 0:DH], bank[n % 3][:].rearrange("p (h d) -> p h d", d=DH),
                                   ACT.Copy).then_inc(a_took.sem, 1)

            def null_exps(g):
                act.wait_ge(a_nullc.sem, a_nullc.at(g, 3))
                act.activation(null_p[:], null_s[:], ACT.Exp).then_inc(a_nexp.sem, 1)

            def score_exps(g, h):
                if h >= 2:
                    act.wait_ge(a_pv.sem, a_pv.at(g, h - 1))
                act.wait_ge(a_s.sem, a_s.at(g, 2 * h + 1))
                act.activation(p_diag[:, h % 2, :], bank[h % 2][:], ACT.Exp, bias=bias_diag[:, h:h + 1],
                               scale=8.0).then_inc(a_exp.sem, 1)
                act.wait_ge(a_s.sem, a_s.at(g, 2 * h + 2))
                act.activation(p_off[:, h % 2, :], bank[2][:, 0:2 * P], ACT.Exp, bias=bias_off[:, h:h + 1],
                               scale=8.0).then_inc(a_exp.sem, 1)

            def out_cols(g, c):
                act.wait_ge(a_oT.sem, a_oT.at(g, c + 1))
                if c < 8:
                    act.activation(outT[:, c, :], bank[7 if c < 7 else 0][:], ACT.Copy).then_inc(a_oc.sem, 1)
                else:
                    act.activation(null_pT, bank[1][0:H * NULLS, :], ACT.Copy).then_inc(a_oc.sem, 1)

            def f_apply(g):
                act.wait_ge(f_turned.sem, f_turned.at(g))
                act.activation(xmT[:], bank[4][:], ACT.Copy).then_inc(f_cols.sem, 1)

            def f_route(g):
                act.wait_ge(f_pick.sem, f_pick.at(g, 2 + 2 * T))
                act.activation(gap1[:], gap1[:], ACT.Tanh, scale=0.5).then_inc(f_gap.sem, 1)

            def f_sw(g, j):
                act.wait_ge(f_gu.sem, f_gu.at(g, j + 1))
                act.activation(tanh1[:], bank[4][:], ACT.Tanh, scale=0.5).then_inc(f_tanh.sem, 1)

            def f_me_(g, j):
                act.wait_ge(f_me.sem, f_me.at(g, j + 1))
                act.activation(hid_me[j], bank[7][:], ACT.Gelu, bias=b_me[:, j:j + 1]).then_inc(f_meg.sem, 1)

            def f_ml_(g, j):
                act.wait_ge(f_ml.sem, f_ml.at(g, j + 1))
                if j == 0 and not (known(g) and g == G - 1):
                    act.wait_ge(a_ss.sem, a_ss.at(g + 1))
                act.activation(hid_ml[j], bank[4 + j % 2][:], ACT.Gelu, bias=b_ml[:, j:j + 1]).then_inc(f_mlg.sem, 1)

            def f_ce_apply(g):
                act.wait_ge(f_ce.sem, f_ce.at(g, 2))
                act.activation(ce_T, bank[6][:], ACT.Copy).then_inc(f_cec.sem, 1)

            def f_relu_(g, j):
                act.wait_ge(f_r.sem, f_r.at(g, j + 1))
                act.activation(hid_relu[j], bank[6 + j][:], ACT.Relu, bias=b_f1[:, j:j + 1]).then_inc(f_relu.sem, 1)

            def f_ce2_apply(g):
                act.wait_ge(f_gT.sem, f_gT.at(g))
                act.activation(ce_T, bank[6][:], ACT.Copy).then_inc(f_cec.sem, 1)

            plan(act, {
                "s_turn": s_turn, "s_fold1": s_fold1, "s_fold2": s_fold2, "s_fold3": s_fold3,
                "l_turn3": to_cols, "l_exp": exps0, "l_ct": coef_cols, "l_g": tanh_l,
                "l_x": xa_cols, "a_m": projected, "a_t": flat, "a_v": values, "a_nexp": null_exps,
                "a_scores": score_exps, "a_ot": out_cols,
                "f_turn": f_apply, "f_pick": f_route, "f_sw": f_sw, "f_me": f_me_, "f_ml": f_ml_,
                "f_cet": f_ce_apply, "f_relu": f_relu_, "f_ce2t": f_ce2_apply,
            })

        @block.vector
        def _(dve):
            n = [0]

            def link(i):
                n[0] += 1
                i.then_inc(made, 1)
                dve.wait_ge(made, n[0])

            def split(w, full):
                link(V.tensor_copy(w.hi, full))
                link(V.tensor_tensor(w.lo, full, w.hi.bitcast(F32), ALU.subtract))

            V = nc.vector
            def s_phase():
                dve.wait_ge(act_made, 1)
                link(V.tensor_tensor(col["z"], col["decay"], col["scale"], ALU.mult))
                link(V.tensor_scalar(col["nz"], col["z"], -1.0, None, ALU.mult))
                dve.sem_inc(z_made, 1)
                link(V.tensor_tensor(col["theta"], col["angle"], col["scale"], ALU.mult))
                dve.wait_ge(pool_made, POOL_MADE)
                link(V.tensor_scalar(phase, time, col["theta"], 1.0 / TWO_PI, ALU.mult, ALU.mult))
                for shift, dst in ((0.0, part_a), (0.25, part_b)):
                    link(V.tensor_scalar(frac, phase, shift, None, ALU.add))
                    link(V.tensor_scalar(turns, frac, ROUND, None, ALU.add))
                    link(V.tensor_scalar(turns, turns, -ROUND, None, ALU.add))
                    link(V.tensor_tensor(frac, frac, turns, ALU.subtract))
                    link(V.tensor_scalar(dst, frac, 0.4999999, -0.4999999, ALU.min, ALU.max))
                dve.sem_inc(phase_made, 1)

            def s_conv():
                dve.wait_ge(act_made, 5)
                link(V.tensor_scalar(col["gate"], col["r"], -1.0, 1.0, ALU.mult, ALU.add))
                c0, s0 = cos_t[:, 0:L], sin_t[:, 0:L]
                link(V.tensor_scalar(part_a[:, 0:L], s0, col["init_im"], None, ALU.mult))
                link(V.scalar_tensor_tensor(out=part_a[:, 0:L], in0=c0, scalar=col["init_re"], in1=part_a[:, 0:L], op0=ALU.mult, op1=ALU.subtract))
                link(V.tensor_scalar(conv_a[:], part_a[:, 0:L], col["gate"], None, ALU.mult))
                link(V.tensor_scalar(part_b[:, 0:L], c0, col["init_im"], None, ALU.mult))
                link(V.scalar_tensor_tensor(out=part_b[:, 0:L], in0=s0, scalar=col["init_re"], in1=part_b[:, 0:L], op0=ALU.mult, op1=ALU.add))
                link(V.tensor_scalar(conv_b[:], part_b[:, 0:L], col["gate"], None, ALU.mult))
                c1, s1 = cos_t[:, 1:L + 1], sin_t[:, 1:L + 1]
                link(V.tensor_scalar(part_a[:, 0:L], s1, col["last_im"], None, ALU.mult))
                link(V.scalar_tensor_tensor(out=part_a[:, 0:L], in0=c1, scalar=col["last_re"], in1=part_a[:, 0:L], op0=ALU.mult, op1=ALU.subtract))
                link(V.tensor_tensor(part_a[:, 0:L], part_a[:, 0:L], rpow[:, 1:L + 1], ALU.mult))
                link(V.tensor_scalar(conv_c[:], part_a[:, 0:L], col["gate"], None, ALU.mult))
                dr = decay_row[:].rearrange("p (s t) -> p s t", s=SEQ)
                link(V.tensor_scalar(dr, time[:, 0:L].unsqueeze(1).to_broadcast([P, SEQ, L]), 0.0, col["r"], ALU.mult, ALU.add))
                link(V.memset(dr[:, :, 0:1], 0.0))

            def s_alibi():
                link(V.tensor_scalar(zraw[:, 0:1], part_no[:], -float(MID), None, ALU.add))
                link(V.tensor_scalar(zraw[:, 1:2], part_no[:], -float(MID + P), None, ALU.add))
                link(V.tensor_scalar(bias_diag[:], slope[:], zraw[:, 0:1], None, ALU.mult))
                link(V.tensor_scalar(bias_off[:], slope[:], zraw[:, 1:2], None, ALU.mult))
                for t in range(T):
                    for k in range(NULLS):
                        link(V.tensor_scalar(bias_null[:, t, :, k], slope[:], float(k - NULLS - MID - P * (t % 2)), None, ALU.mult))

            def s_w0():
                dve.wait_ge(loaded1, 16 * 7)
                link(V.tensor_scalar(w0_down[:], w0_down[:], 0.5, None, ALU.mult))
                for w, full in ((w0_router, w0_router_raw), (w0_gate, w0_gate_raw), (w0_up, w0_up_raw)):
                    split(w, full)
                link(V.tensor_copy(sel[:], sel_f))
                link(V.tensor_scalar(coef0[:], sel_f, 0.0, None, ALU.mult))
                dve.sem_inc(w0_made, 1)

            def s_scale():
                dve.wait_ge(loaded2, 16 * LOADS2)
                dve.wait_ge(loaded3, 16 * LOADS3)
                link(V.tensor_scalar(w_sw2[:], w_sw2[:], 0.5, None, ALU.mult))
                link(V.tensor_scalar(w_q_raw, w_q_raw, col["gamma"], None, ALU.mult))
                link(V.tensor_scalar(w_kv_raw, w_kv_raw, col["gamma"], None, ALU.mult))
                link(V.tensor_tensor(qk_scale[:], col["qs"], col["ks"], ALU.mult))
                link(V.tensor_tensor(b1_router[:, 0:E1], b1_router[:, 0:E1], lb_row[:, 0:E1], ALU.add))
                link(V.tensor_tensor(qs_row, qs_row, ks_row, ALU.mult))
                link(V.tensor_tensor(nk_sq, nk_rows, nk_rows, ALU.mult))
                link(V.tensor_reduce(nk_ss[:, 0:1], nk_sq, AX_X, ALU.add))
                link(V.tensor_scalar(nk_ss[:, 0:1], nk_ss[:, 0:1], 1e-24, None, ALU.max))
                dve.sem_inc(nk_summed, 1)

            def s_raw():
                link(V.tensor_scalar(par_i[:], par_i[:], 1, 1, ALU.logical_shift_right, ALU.bitwise_and))
                link(V.tensor_copy(par[:, 1:2], par_i[:, 0:1]))
                link(V.tensor_scalar(par[:, 0:1], par[:, 1:2], -1.0, 1.0, ALU.mult, ALU.add))
                dve.wait_ge(pool_made, POOL_MADE + 1)
                link(V.tensor_scalar(nk_rows, nk_rows, nk_ss[:, 1:2], None, ALU.mult))
                link(V.tensor_tensor(nk_rows, nk_rows, qs_row, ALU.mult))
                for s in range(2):
                    link(V.tensor_scalar(nk_z[:, 64 * s:64 * s + 64], nk_rows, par[:, s:s + 1], None, ALU.mult))
                    link(V.tensor_scalar(nv_z[:, 64 * s:64 * s + 64], nv_rows, par[:, s:s + 1], None, ALU.mult))
                link(V.tensor_copy(colb[0], col["syn_b"].to_broadcast([P, P])))
                link(V.tensor_copy(colb[1], col["ce_bv"].to_broadcast([P, P])))
                link(V.tensor_copy(colb[2], col["n2b"].to_broadcast([P, P])))
                dve.sem_inc(raw_made, 1)

            def s_pad():
                dve.wait_ge(act_made, 7)
                for c in range(8):
                    link(V.tensor_copy(nv_pad[:, c, 4 * c:4 * c + 4], nv_zT[:, 4 * c:4 * c + 4]))
                dve.sem_inc(pad_made, 1)

            def s_v2():
                dve.wait_ge(pe_made, 5)
                link(V.tensor_tensor(ce_v2, bank[7][:, 384:512], ident[:], ALU.add))
                dve.sem_inc(v2_made, 1)

            def s_bias():
                dve.wait_ge(pe_made, 9)
                link(V.tensor_copy(w_ce[:], bank[0][:, 0:P]))
                link(V.tensor_tensor(row_ce[:], bank[0][:, P:2 * P], row_tmp[0], ALU.add))
                link(V.tensor_tensor(row_out[:, 2, :], bank[0][:, 2 * P:3 * P], row_tmp[2], ALU.add))
                link(V.tensor_tensor(row_res[:], row_tmp[1], row_tmp[3], ALU.add))
                link(V.tensor_tensor(b_me[:], bank[7][:, 0:2], c1b, ALU.add))
                link(V.tensor_tensor(b_f1[:], bank[7][:, 2:4], f1b, ALU.add))
                split(w_nk, bank[7][:, 8:8 + H * NULLS])
                link(V.tensor_copy(w_nv[:], bank[7][0:H * NULLS, 128:128 + P]))
                link(V.tensor_scalar(w_f1[:], w_f1[:], col["n1g"], None, ALU.mult))
                link(V.tensor_scalar(w_gen[:], w_gen[:], col["n2g"], None, ALU.mult))

            def s_split():
                dve.wait_ge(act_made, ACT_MADE)
                for w, full in ((w_q, w_q_raw), (w_kv, w_kv_raw)):
                    split(w, full)
                dve.sem_inc(all_set, 1)

            def stats(norm, g, tile):
                s = norm.steps
                for t in range(T):
                    V.bn_stats(norm.six[:, t, :], tile(t)).then_inc(s.sem, 1)
                dve.wait_ge(s.sem, s.at(g, 4))
                dve.sem_inc(dve_passed, 1)
                for t in range(T):
                    V.bn_aggr(norm.mv[:, t, :], norm.six[:, t, :]).then_inc(s.sem, 1)
                dve.wait_ge(s.sem, s.at(g, 8))
                V.tensor_scalar(norm.var[:], norm.mv[:, :, 1], norm.scale, norm.add, ALU.mult, ALU.add).then_inc(s.sem, 1)

            def apply(norm, g, dst, tile):
                dve.wait_ge(norm.rooted.sem, norm.rooted.at(g))
                for t in range(T):
                    V.tensor_scalar(dst[:, t, :], tile(t), norm.mv[:, t, 0:1], norm.rstd[:, t:t + 1],
                                    ALU.subtract, ALU.mult).then_inc(norm.steps.sem, 1)

            def add_residual(norm, g, dst, normed, res):
                dve.wait_ge(norm.steps.sem, norm.steps.at(g, 13))
                V.tensor_tensor(dst[:], normed[:], res[:], ALU.add).then_inc(norm.steps.sem, 1)

            def e_stats(g):
                dve.wait_ge(x_loaded.sem, x_loaded.at(g))
                stats(n_x, g, lambda t: xin[:, t, :])

            def e_apply(g):
                apply(n_x, g, xn, lambda t: xin[:, t, :])

            def e_scan(g):
                dve.wait_ge(l_turned.sem, l_turned.at(g, 1))
                for k, w in enumerate((cos_t, sin_t)):
                    V.tensor_tensor(conv[:, k, :].rearrange("p (s t) -> p s t", s=SEQ),
                                    bank[7][:].rearrange("p (s t) -> p s t", s=SEQ),
                                    w[:, 0:L].unsqueeze(1).to_broadcast([P, SEQ, L]), ALU.mult).then_inc(l_conv.sem, 1)
                for k in range(2):
                    dve.wait_ge(l_conv.sem, l_conv.at(g, 1 + k))
                    V.tensor_tensor_scan(conv[:, 2 + k, :], decay_row[:], conv[:, k, :], 0.0, ALU.mult, ALU.add).then_inc(l_conv.sem, 1)

            def e_sum(g):
                dve.wait_ge(l_gain.sem, l_gain.at(g))
                V.tensor_tensor(conv[:, 0, :], conv[:, 0, :], conv[:, 1, :], ALU.add).then_inc(l_conv.sem, 1)
                dve.wait_ge(l_conv.sem, l_conv.at(g, 5))
                V.tensor_tensor(conv[:, 0, :].rearrange("p (s t) -> p s t", s=SEQ),
                                conv[:, 0, :].rearrange("p (s t) -> p s t", s=SEQ),
                                conv_c[:].unsqueeze(1).to_broadcast([P, SEQ, L]), ALU.add).then_inc(l_conv.sem, 1)

            def l_turn2(g):
                dve.wait_ge(l_turned.sem, l_turned.at(g, 2))
                stats(n_y, g, lambda t: bank[3][:, t * P:(t + 1) * P])

            def l_res(g):
                apply(n_y, g, xn, lambda t: bank[3][:, t * P:(t + 1) * P])
                add_residual(n_y, g, x1, xn, xin)
                dve.wait_ge(n_y.steps.sem, n_y.steps.at(g))
                stats(n_l, g, lambda t: x1[:, t, :])

            def l_norm(g):
                apply(n_l, g, xn, lambda t: x1[:, t, :])

            def low(part, full):
                V.tensor_tensor(part.lo, full, part.hi.bitcast(F32), ALU.subtract).then_inc(l_low.sem, 1)

            def l_turn3(g):
                dve.wait_ge(l_cols.sem, l_cols.at(g, 1))
                low(xlT, bank[3][:])

            def l_cT(g):
                dve.wait_ge(l_cols.sem, l_cols.at(g, 2))
                low(coef0T, bank[6][0:E0, :])

            def l_xl(g):
                dve.wait_ge(l_xc.sem, l_xc.at(g))
                low(xaT, bank[5][:])

            def l_route(g):
                s = l_pick
                dve.wait_ge(l_routed.sem, l_routed.at(g, 1))
                V.tensor_copy(logit0[:], bank[3][:, 0:T * 8].rearrange("p (t e) -> p t e", e=8)).then_inc(s.sem, 1)

            def l_pick_(g):
                s = l_pick
                dve.wait_ge(s.sem, s.at(g, 1))
                dve.sem_inc(dve_passed, 1)
                for t in range(T):
                    V.max(top0[:, t, :], logit0[:, t, :]).then_inc(s.sem, 1)
                dve.wait_ge(s.sem, s.at(g, 1 + T))
                dve.sem_inc(dve_passed, 1)
                for t in range(T):
                    V.max_index(idx0[:, t, :], top0[:, t, :], logit0[:, t, :]).then_inc(s.sem, 1)
                V.tensor_tensor(exp0[:], top0[:], top0[:, :, 0:1].to_broadcast([P, T, 8]), ALU.subtract).then_inc(s.sem, 1)

            def l_coef(g):
                s = l_pick
                k = 2 + 2 * T
                dve.wait_ge(s.sem, s.at(g, k))
                V.tensor_copy(idf0[:], idx0[:, :, 0:2]).then_inc(s.sem, 1)
                dve.wait_ge(l_exp.sem, l_exp.at(g))
                V.tensor_reduce(sum0[:], exp0[:], AX_X, ALU.add).then_inc(s.sem, 1)
                dve.wait_ge(s.sem, s.at(g, k + 2))
                V.reciprocal(sum0[:], sum0[:]).then_inc(s.sem, 1)
                for j in range(2):
                    V.tensor_tensor(pick0[:, j, :, :], expert_no[:], idf0[:, :, j:j + 1].to_broadcast([P, T, 8]), ALU.is_equal).then_inc(s.sem, 1)
                dve.wait_ge(s.sem, s.at(g, k + 3))
                V.tensor_tensor(prob0[:], exp0[:, :, 0:2], sum0[:].unsqueeze(2).to_broadcast([P, T, 2]), ALU.mult).then_inc(s.sem, 1)
                dve.wait_ge(s.sem, s.at(g, k + 6))
                for j in range(2):
                    V.tensor_tensor(pick0[:, j, :, :], pick0[:, j, :, :], prob0[:, :, j:j + 1].to_broadcast([P, T, 8]), ALU.mult).then_inc(s.sem, 1)
                dve.wait_ge(s.sem, s.at(g, k + 8))
                V.tensor_tensor(pick0[:, 0, :, :], pick0[:, 0, :, :], pick0[:, 1, :, :], ALU.add).then_inc(l_coefd.sem, 1)

            def l_hg_(g, j):
                dve.wait_ge(l_tanh.sem, l_tanh.at(g, j + 1))
                V.scalar_tensor_tensor(out=hid0[:, j, :], in0=tanh0, scalar=1.0, in1=bank[4][:], op0=ALU.add, op1=ALU.mult).then_inc(l_hg.sem, 1)

            def l_hu_(g, j):
                dve.wait_ge(l_u.sem, l_u.at(g, j + 1))
                dve.wait_ge(l_hg.sem, l_hg.at(g, j + 1))
                V.tensor_tensor(hid0[:, j, :], hid0[:, j, :], bank[5][:], ALU.mult).then_inc(l_hu.sem, 1)

            def l_hc_(g, j):
                dve.wait_ge(l_c.sem, l_c.at(g, j + 1))
                dve.wait_ge(l_hu.sem, l_hu.at(g, j + 1))
                V.tensor_tensor(hid0[:, j, :], hid0[:, j, :], bank[6][:], ALU.mult).then_inc(l_hc.sem, 1)

            def l_down_(g):
                dve.wait_ge(l_down.sem, l_down.at(g))
                stats(n_d, g, lambda t: bank[4][:, t * P:(t + 1) * P])

            def l_end(g):
                apply(n_d, g, xn, lambda t: bank[4][:, t * P:(t + 1) * P])
                if not first(g):
                    dve.wait_ge(a_kept.sem, a_kept.at(g - 1))
                add_residual(n_d, g, x2n, xn, x1)

            def a_stats(g):
                dve.wait_ge(n_d.steps.sem, n_d.steps.at(g))
                stats(n_a, g, lambda t: x2n[:, t, :])

            def a_apply(g):
                apply(n_a, g, xa, lambda t: x2n[:, t, :])

            def a_null(g):
                dve.wait_ge(a_nulls.sem, a_nulls.at(g))
                V.tensor_copy(null_s[:], bank[3][:, 0:T * H * NULLS].rearrange("p (t h n) -> p t h n", h=H, n=NULLS)).then_inc(a_nullc.sem, 1)

            def a_sums(g, t, k):
                s = a_ss
                dve.wait_ge(a_sq.sem, a_sq.at(g, 4 * t + 2 * k + 2))
                if t >= 2:
                    dve.wait_ge(a_root.sem, a_root.at(g, 2 * (t - 2) + k + 1))
                elif not first(g):
                    dve.wait_ge(a_root.sem, a_root.at(g - 1, 2 * (t + 2) + k + 1))
                V.tensor_reduce(sumsq[:, t % 2, k, :], square[:, 2 * k:2 * k + 2, :].rearrange("p j (h d) -> p (j h) d", d=DH),
                                AX_X, ALU.add).then_inc(s.sem, 1)
                dve.wait_ge(s.sem, s.at(g, 4 * t + 2 * k + 1))
                V.tensor_scalar(sumsq[:, t % 2, k, :], sumsq[:, t % 2, k, :], 1e-24, None, ALU.max).then_inc(s.sem, 1)

            def a_units(g, t, k):
                dve.wait_ge(a_root.sem, a_root.at(g, 2 * t + k + 1))
                dve.wait_ge(a_took.sem, a_took.at(g, use("m", t, 2 * k + 1) + 1))
                raw = unit[:, t % 2, 2 * k:2 * k + 2, :].rearrange("p j (h d) -> p (j h) d", d=DH)
                V.tensor_tensor(raw, raw, rnorm[:, k, t, :].unsqueeze(2).to_broadcast([P, H, DH]), ALU.mult).then_inc(a_unit.sem, 1)

            def a_nexp_(g):
                dve.wait_ge(a_nullc.sem, a_nullc.at(g, 1))
                V.tensor_tensor(null_s[:], null_s[:], rnorm[:, 1, :, :].unsqueeze(3).to_broadcast([P, T, H, NULLS]), ALU.mult).then_inc(a_nullc.sem, 1)
                dve.wait_ge(a_nullc.sem, a_nullc.at(g, 2))
                V.scalar_tensor_tensor(out=null_s[:].rearrange("p t h n -> p (t h n)"), in0=null_s[:].rearrange("p t h n -> p (t h n)"),
                                       scalar=8.0, in1=bias_null[:].rearrange("p t h n -> p (t h n)"),
                                       op0=ALU.mult, op1=ALU.add).then_inc(a_nullc.sem, 1)
                dve.wait_ge(a_nexp.sem, a_nexp.at(g))
                V.tensor_tensor(null_sum[:], null_p[:, :, :, 0], null_p[:, :, :, 1], ALU.add).then_inc(a_nullc.sem, 1)

            def a_mixes(g, h):
                s = a_mix
                pv = bank[3][:, 0:T * (DH + 1)].rearrange("p (t d) -> p t d", t=T)
                dve.wait_ge(a_pv.sem, a_pv.at(g, h + 1))
                if h == 0:
                    dve.wait_ge(a_nullc.sem, a_nullc.at(g, 4))
                V.tensor_tensor(denom[:], pv[:, :, DH], null_sum[:, :, h], ALU.add).then_inc(s.sem, 1)
                dve.wait_ge(s.sem, s.at(g, 3 * h + 1))
                V.reciprocal(recip[:, :, h], denom[:]).then_inc(s.sem, 1)
                dve.wait_ge(s.sem, s.at(g, 3 * h + 2))
                V.tensor_tensor(mixed[:, :, h * DH:(h + 1) * DH], pv[:, :, 0:DH],
                                recip[:, :, h:h + 1].to_broadcast([P, T, DH]), ALU.mult).then_inc(s.sem, 1)
                if h == H - 1:
                    V.tensor_tensor(null_p[:], null_p[:], recip[:].unsqueeze(3).to_broadcast([P, T, H, NULLS]), ALU.mult).then_inc(a_pn.sem, 1)

            def a_out_(g):
                dve.wait_ge(a_out.sem, a_out.at(g))
                stats(n_o, g, lambda t: bank[3][:, t * P:(t + 1) * P])

            def a_end(g):
                if not first(g):
                    dve.wait_ge(n_f.steps.sem, n_f.steps.at(g - 1))
                apply(n_o, g, x3, lambda t: bank[3][:, t * P:(t + 1) * P])
                dve.wait_ge(a_kept.sem, a_kept.at(g))
                add_residual(n_o, g, x3, x3, x2)

            def f_stats(g):
                dve.wait_ge(n_o.steps.sem, n_o.steps.at(g))
                stats(n_m, g, lambda t: x3[:, t, :])

            def f_apply(g):
                apply(n_m, g, x4m, lambda t: x3[:, t, :])

            def f_ce_(g):
                dve.wait_ge(f_ce.sem, f_ce.at(g, 1))
                V.tensor_tensor(ce_rows[:], rows3(bank[6][:]), row_ce[:].unsqueeze(1).to_broadcast([P, T, D]), ALU.add).then_inc(f_ced.sem, 1)
                dve.wait_ge(f_ced.sem, f_ced.at(g, 1))
                stats(n_c, g, lambda t: ce_rows[:, t, :])

            def f_ce_apply(g):
                apply(n_c, g, ce_rows, lambda t: ce_rows[:, t, :])

            def f_ce2(g):
                dve.wait_ge(f_ce.sem, f_ce.at(g, 3))
                dve.wait_ge(f_res.sem, f_res.at(g))
                V.tensor_tensor(ce_rows[:], rows3(bank[6][:]), ce_res, ALU.add).then_inc(f_ced.sem, 1)
                dve.wait_ge(f_ced.sem, f_ced.at(g, 2))
                stats(n_c2, g, lambda t: ce_rows[:, t, :])

            def f_ce2_apply(g):
                apply(n_c2, g, ce_rows, lambda t: ce_rows[:, t, :])

            def f_route(g):
                s = f_pick
                dve.wait_ge(f_routed.sem, f_routed.at(g))
                V.tensor_tensor(logit1[:], bank[7][:, 0:T * 8].rearrange("p (t e) -> p t e", e=8),
                                b1_router[:].unsqueeze(1).to_broadcast([P, T, 8]), ALU.add).then_inc(s.sem, 1)
                dve.wait_ge(s.sem, s.at(g, 1))
                dve.sem_inc(dve_passed, 1)
                for t in range(T):
                    V.max(top1[:, t, :], logit1[:, t, :]).then_inc(s.sem, 1)
                dve.wait_ge(s.sem, s.at(g, 1 + T))
                dve.sem_inc(dve_passed, 1)
                for t in range(T):
                    V.max_index(idx1[:, t, :], top1[:, t, :], logit1[:, t, :]).then_inc(s.sem, 1)
                V.tensor_tensor(gap1[:], top1[:, :, 1], top1[:, :, 0], ALU.subtract).then_inc(s.sem, 1)

            def f_pick_(g):
                s = f_pick
                k = 2 + 2 * T
                dve.wait_ge(s.sem, s.at(g, k))
                V.tensor_copy(idf1[:], idx1[:, :, 0:2]).then_inc(s.sem, 1)
                dve.wait_ge(f_gap.sem, f_gap.at(g))
                V.tensor_scalar(wt1[:, :, 0], gap1[:], -0.5, 0.5, ALU.mult, ALU.add).then_inc(s.sem, 1)
                V.tensor_scalar(wt1[:, :, 1], gap1[:], 0.5, 0.5, ALU.mult, ALU.add).then_inc(s.sem, 1)
                dve.wait_ge(s.sem, s.at(g, k + 1))
                for j in range(2):
                    V.tensor_tensor(pick1[:, j, :, :], expert_no[:], idf1[:, :, j:j + 1].to_broadcast([P, T, 8]), ALU.is_equal).then_inc(s.sem, 1)
                dve.wait_ge(s.sem, s.at(g, k + 5))
                for j in range(2):
                    V.tensor_tensor(pick1[:, j, :, :], pick1[:, j, :, :], wt1[:, :, j:j + 1].to_broadcast([P, T, 8]), ALU.mult).then_inc(s.sem, 1)
                dve.wait_ge(s.sem, s.at(g, k + 7))
                V.tensor_tensor(pick1[:, 0, :, :], pick1[:, 0, :, :], pick1[:, 1, :, :], ALU.add).then_inc(f_coefd.sem, 1)

            def f_sw(g, j):
                s = f_hid
                dve.wait_ge(f_tanh.sem, f_tanh.at(g, j + 1))
                V.scalar_tensor_tensor(out=hid_sw[j], in0=tanh1[:], scalar=1.0, in1=bank[4][:], op0=ALU.add, op1=ALU.mult).then_inc(s.sem, 1)
                dve.wait_ge(s.sem, s.at(g, 2 * j + 1))
                V.tensor_tensor(hid_sw[j], hid_sw[j], bank[5][:], ALU.mult).then_inc(s.sem, 1)

            def f_out(g, t):
                dve.wait_ge(f_e.sem, f_e.at(g, t + 1))
                if t == 0:
                    dve.wait_ge(f_bias.sem, f_bias.at(g))
                for e in range(E1):
                    if e:
                        dve.wait_ge(f_eb.sem, f_eb.at(g, E1 * t + e))
                    V.scalar_tensor_tensor(out=x4m[:, t, :], in0=bank[4 + t][:, e * P:(e + 1) * P], scalar=pick1[:, 0, t, e:e + 1],
                                           in1=x4m[:, t, :] if e else mix_bias[:, t, :], op0=ALU.mult, op1=ALU.add).then_inc(f_eb.sem, 1)

            def f_end_stats(g):
                dve.wait_ge(f_eb.sem, f_eb.at(g))
                stats(n_f, g, lambda t: x4m[:, t, :])

            def f_end(g):
                apply(n_f, g, x4m, lambda t: x4m[:, t, :])
                dve.wait_ge(stored.sem, stored.at(g))
                add_residual(n_f, g, x4, x4m, x3)

            plan(dve, {
                "s_phase": s_phase, "s_conv": s_conv, "s_alibi": s_alibi, "s_w0": s_w0, "s_scale": s_scale, "s_raw": s_raw,
                "s_pad": s_pad, "s_v2": s_v2, "s_bias": s_bias, "s_split": s_split,
                "e_stats": e_stats, "e_apply": e_apply, "e_scan": e_scan, "e_sum": e_sum, "l_turn2": l_turn2, "l_res": l_res,
                "l_norm": l_norm, "l_turn3": l_turn3, "l_ct": l_cT, "l_xl": l_xl, "l_route": l_route, "l_pick": l_pick_, "l_coef": l_coef, "l_hg": l_hg_, "l_hu": l_hu_,
                "l_hc": l_hc_, "l_dstats": l_down_, "l_end": l_end, "l_astats": a_stats, "l_aapply": a_apply,
                "a_null": a_null, "a_ss": a_sums, "a_u": a_units,
                "a_nexp": a_nexp_, "a_mix": a_mixes, "a_o": a_out_, "a_end": a_end,
                "f_stats": f_stats, "f_apply": f_apply, "f_route": f_route, "f_pick": f_pick_, "f_ce": f_ce_,
                "f_ce_apply": f_ce_apply, "f_ce2": f_ce2, "f_ce2_apply": f_ce2_apply, "f_hid": f_sw, "f_out": f_out,
                "f_end_stats": f_end_stats, "f_end": f_end,
            })

        @block.tensor
        def _(pe):
            mm = nc.tensor.matmul

            def mm3(dst, left, right):
                mm(dst, left.hi, right.hi, start=True, stop=False)
                mm(dst, left.hi, right.lo, start=False, stop=False)
                return mm(dst, left.lo, right.hi, start=False, stop=True)

            def turn(dst, src):
                for t in range(4):
                    last = nc.tensor.transpose(dst[:, t * P:(t + 1) * P], src(t), ident[:])
                return last

            pe.wait_ge(pool_made, POOL_MADE)

            def s_w0():
                pe.wait_ge(w0_made, 1)

            def s_turn():
                pe.wait_ge(raw_made, 1)
                nc.tensor.transpose(bank[0][:, 0:32], nk_z, ident[0:32, 0:32])
                nc.tensor.transpose(bank[0][:, 32:64], nv_z, ident[0:32, 0:32])
                for i in range(2):
                    last = nc.tensor.transpose(bank[0][:, (i + 1) * P:(i + 2) * P], ce_raw[i], ident[:])
                last.then_inc(pe_made, 1)
                for k in range(2):
                    turn(bank[1 + k], lambda t: w_q_raw[:, (4 * k + t) * P:(4 * k + t + 1) * P]).then_inc(pe_made, 1)
                for i in range(3):
                    last = nc.tensor.transpose(bank[7][:, i * P:(i + 1) * P], me_raw[i], ident[:])
                last.then_inc(pe_made, 1)

            def s_fold1():
                pe.wait_ge(act_made, 14)
                mm(bank[7][:, 3 * P:], wT[5], ce_raw[2], start=True, stop=True).then_inc(pe_made, 1)
                mm(bank[1][:, 0:2 * P], wT[2], me_c1, start=True, stop=True).then_inc(pe_made, 1)

            def s_fold2():
                pe.wait_ge(act_made, 15)
                mm(bank[1][:, 2 * P:], wT[1], me_p1, start=True, stop=True).then_inc(pe_made, 1)

            def s_fold3():
                pe.wait_ge(act_made, 16)
                mm(bank[2][:, 0:2 * P], wT[0], me_p2, start=True, stop=True).then_inc(pe_made, 1)

            def s_fold4():
                pe.wait_ge(v2_made, 1)
                pe.wait_ge(pad_made, 1)
                mm(bank[0][:, 0:P], wT[4], ce_v2, start=True, stop=True)
                mm(bank[0][:, P:2 * P], colb[0], ce_v2, start=True, stop=False)
                mm(bank[0][:, P:2 * P], colb[1], ce_raw[2], start=False, stop=True)
                mm(bank[0][:, 2 * P:3 * P], colb[2], w_gen[:], start=True, stop=True)
                for j in range(2):
                    js = slice(j * P, (j + 1) * P)
                    mm(bank[7][:, j:j + 1], me_c1[:, js], col["me_bo"], start=True, stop=False)
                    mm(bank[7][:, j:j + 1], me_p1[:, js], col["me_bv"], start=False, stop=False)
                    mm(bank[7][:, j:j + 1], me_p2[:, js], col["eq_b"], start=False, stop=True)
                for j in range(2):
                    mm(bank[7][:, 2 + j:3 + j], w_f1[:, j * P:(j + 1) * P], col["n1b"], start=True, stop=True)
                for c in range(8):
                    mm(bank[7][:, 8 + 4 * c:12 + 4 * c], wqT[:, c, :], nk_zT[:, 4 * c:4 * c + 4], start=True, stop=True)
                for c in range(8):
                    last = mm(bank[7][0:H * NULLS, P:2 * P], nv_pad[:, c, :], w_out[:, c, :], start=(c == 0), stop=(c == 7))
                last.then_inc(pe_made, 1)

            def s_split():
                pe.wait_ge(all_set, 1)

            def e_turn1(g):
                pe.wait_ge(n_x.steps.sem, n_x.steps.at(g))
                if known(g) and g == 1:
                    pe.wait_ge(all_set, 1)
                elif not (known(g) and g < 3):
                    pe.wait_ge(f_eb.sem, f_eb.at(g - 3))
                turn(bank[7], lambda t: xn[:, t, :]).then_inc(l_turned.sem, 1)

            def l_turn2(g):
                pe.wait_ge(l_conv.sem, l_conv.at(g))
                turn(bank[3], lambda t: conv[:, 0, t * P:(t + 1) * P]).then_inc(l_turned.sem, 1)

            def l_turn3(g):
                pe.wait_ge(n_l.steps.sem, n_l.steps.at(g))
                turn(bank[3], lambda t: xn[:, t, :]).then_inc(l_turned.sem, 1)

            def l_route(g):
                pe.wait_ge(l_low.sem, l_low.at(g, 1))
                for t in range(T):
                    last = mm3(bank[3][:, 8 * t:8 * t + 8], xlT[:, t * P:(t + 1) * P], w0_router)
                last.then_inc(l_routed.sem, 1)

            def without_f(g):
                return known(g) and g < 2

            def l_cT(g):
                pe.wait_ge(l_coefd.sem, l_coefd.at(g))
                if not without_f(g):
                    pe.wait_ge(f_eb.sem, f_eb.at(g - 2, 3 * E1))
                for t in range(T):
                    last = nc.tensor.transpose(bank[6][0:E0, t * P:(t + 1) * P], pick0[:, 0, t, :], ident[:])
                last.then_inc(l_routed.sem, 1)

            def l_g_(g, j):
                if j:
                    pe.wait_ge(l_hg.sem, l_hg.at(g, j))
                elif not without_f(g):
                    pe.wait_ge(f_eb.sem, f_eb.at(g - 2, E1))
                mm3(bank[4][:], w0_gate[:, j * P:(j + 1) * P], xlT).then_inc(l_g.sem, 1)

            def l_u_(g, j):
                if j:
                    pe.wait_ge(l_hu.sem, l_hu.at(g, j))
                elif not without_f(g):
                    pe.wait_ge(f_eb.sem, f_eb.at(g - 2, 2 * E1))
                mm3(bank[5][:], w0_up[:, j * P:(j + 1) * P], xlT).then_inc(l_u.sem, 1)

            def l_c_(g, j):
                if j:
                    pe.wait_ge(l_hc.sem, l_hc.at(g, j))
                else:
                    pe.wait_ge(l_low.sem, l_low.at(g, 2))
                mm(bank[6][:], sel[:, j * P:(j + 1) * P], coef0[:], start=True, stop=True).then_inc(l_c.sem, 1)

            def l_down_(g, t):
                if t == 0:
                    pe.wait_ge(l_hu.sem, l_hu.at(g))
                    pe.wait_ge(l_hc.sem, l_hc.at(g))
                for j in range(J0 + 1):
                    last = mm(bank[4][:, t * P:(t + 1) * P], hid0[:, j, t * P:(t + 1) * P], w0_down[:, j, :],
                              start=(j == 0), stop=(j == J0))
                last.then_inc(l_down.sem, 1)

            def l_x(g):
                pe.wait_ge(n_a.steps.sem, n_a.steps.at(g))
                turn(bank[5], lambda t: xa[:, t, :]).then_inc(l_xt.sem, 1)

            def a_null(g):
                pe.wait_ge(l_low.sem, l_low.at(g))
                if first(g):
                    pe.wait_ge(l_pick.sem, l_pick.at(g, 1))
                else:
                    pe.wait_ge(n_o.steps.sem, n_o.steps.at(g - 1))
                for t in range(T):
                    last = mm3(bank[3][:, 32 * t:32 * t + 32], xaT[:, t * P:(t + 1) * P], w_nk)
                last.then_inc(a_nulls.sem, 1)

            def free(g, n):
                if n >= 3:
                    pe.wait_ge(a_took.sem, a_took.at(g, n - 2))

            def a_m(g, t):
                for k in range(4):
                    n = use("m", t, k)
                    w = (w_kv, w_kv, w_q, w_q)[k][:, 512 * (k % 2):512 * (k % 2) + 512]
                    free(g, n)
                    if t == 0 and k == 0:
                        pe.wait_ge(l_low.sem, l_low.at(g))
                    mm3(bank[n % 3][:], xaT[:, t * P:(t + 1) * P], w).then_inc(a_put.sem, 1)

            def a_t(g, t):
                for k in range(4):
                    n = use("t", t, k)
                    pe.wait_ge(a_unit.sem, a_unit.at(g, 2 * t + k // 2 + 1))
                    free(g, n)
                    turn(bank[n % 3], lambda c: unit[:, t % 2, k, c * P:(c + 1) * P]).then_inc(a_put.sem, 1)

            def a_v(g, t):
                for k in range(2):
                    n = use("v", t, k)
                    free(g, n)
                    mm3(bank[n % 3][:], xaT[:, t * P:(t + 1) * P],
                        w_kv[:, H * DH + 512 * k:H * DH + 512 * k + 512]).then_inc(a_put.sem, 1)

            def a_scores(g, h):
                s, c = h % 2, h // 2
                rs = slice(64 * s, 64 * s + 64)
                if h < 2:
                    pe.wait_ge(a_took.sem, a_took.at(g))
                else:
                    pe.wait_ge(a_exp.sem, a_exp.at(g, 2 * (h - 2) + 1))
                for t in range(T):
                    ts = slice(t * P, (t + 1) * P)
                    last = mm(bank[s][:, ts], kT[rs, c, ts], qT[rs, c, ts], start=True, stop=True)
                last.then_inc(a_s.sem, 1)
                if h:
                    pe.wait_ge(a_exp.sem, a_exp.at(g, 2 * h))
                for b in range(SEQ):
                    last = mm(bank[2][:, b * P:(b + 1) * P], kT[rs, c, 2 * b * P:(2 * b + 1) * P],
                              qT[rs, c, (2 * b + 1) * P:(2 * b + 2) * P], start=True, stop=True)
                last.then_inc(a_s.sem, 1)

            def a_mix_(g, h):
                s = h % 2
                pe.wait_ge(a_mask.sem, a_mask.at(g, h + 1))
                pe.wait_ge(a_exp.sem, a_exp.at(g, 2 * h + 2))
                if h:
                    pe.wait_ge(a_mix.sem, a_mix.at(g, 3 * h))
                elif not (known(g) and g == G - 1):
                    pe.wait_ge(l_pick.sem, l_pick.at(g + 1, 1))
                else:
                    pe.wait_ge(a_nullc.sem, a_nullc.at(g, 1))
                for t in range(T):
                    dst = bank[3][:, t * (DH + 1):(t + 1) * (DH + 1)]
                    last = mm(dst, p_diag[:, s, t * P:(t + 1) * P], val[:, t, h, :], start=True, stop=(t % 2 == 0))
                    if t % 2:
                        last = mm(dst, p_off[:, s, (t // 2) * P:(t // 2 + 1) * P], val[:, t - 1, h, :], start=False, stop=True)
                last.then_inc(a_pv.sem, 1)

            def a_oT_(g, c):
                if c < 8:
                    pe.wait_ge(a_mix.sem, a_mix.at(g, 3 * (2 * c + 2)))
                if 0 < c < 7:
                    pe.wait_ge(a_oc.sem, a_oc.at(g, c))
                elif c == 0 and not (known(g) and g >= G - 2):
                    pe.wait_ge(l_conv.sem, l_conv.at(g + 2, 2))
                elif c == 0:
                    pe.wait_ge(f_eb.sem, f_eb.at(g - 1))
                elif c == 7:
                    pe.wait_ge(a_exp.sem, a_exp.at(g))
                if c < 8:
                    turn(bank[7 if c < 7 else 0], lambda t: mixed[:, t, c * P:(c + 1) * P]).then_inc(a_oT.sem, 1)
                else:
                    pe.wait_ge(a_pn.sem, a_pn.at(g))
                    for t in range(T):
                        last = nc.tensor.transpose(bank[1][0:H * NULLS, t * P:(t + 1) * P],
                                                   null_p[:, t, :, :].rearrange("p h n -> p (h n)"), ident[:])
                    last.then_inc(a_oT.sem, 1)

            def a_out_(g):
                pe.wait_ge(a_oc.sem, a_oc.at(g))
                for t in range(T):
                    ts = slice(t * P, (t + 1) * P)
                    for c in range(8):
                        mm(bank[3][:, ts], outT[:, c, ts], w_out[:, c, :], start=(c == 0), stop=False)
                    last = mm(bank[3][:, ts], null_pT[:, ts], w_nv[:], start=False, stop=True)
                last.then_inc(a_out.sem, 1)

            def f_turn(g):
                pe.wait_ge(n_m.steps.sem, n_m.steps.at(g))
                turn(bank[4], lambda t: x4m[:, t, :]).then_inc(f_turned.sem, 1)

            def f_route(g):
                pe.wait_ge(f_cols.sem, f_cols.at(g))
                for t in range(T):
                    last = mm(bank[7][:, 8 * t:8 * t + 8], xmT[:, t * P:(t + 1) * P], w1_router[:], start=True, stop=True)
                last.then_inc(f_routed.sem, 1)

            def f_ce_(g):
                for t in range(T):
                    last = mm(bank[6][:, t * P:(t + 1) * P], xmT[:, t * P:(t + 1) * P], w_ce[:], start=True, stop=True)
                last.then_inc(f_ce.sem, 1)

            def f_sw(g, j):
                js = slice(j * P, (j + 1) * P)
                if j:
                    pe.wait_ge(f_hid.sem, f_hid.at(g, 2 * j))
                mm(bank[4][:], w_sw1[:, js], xmT[:], start=True, stop=True)
                mm(bank[5][:], w_sw3[:, js], xmT[:], start=True, stop=True).then_inc(f_gu.sem, 1)

            def f_me_(g, j):
                js = slice(j * P, (j + 1) * P)
                if j:
                    pe.wait_ge(f_meg.sem, f_meg.at(g, 1))
                    pe.wait_ge(f_relu.sem, f_relu.at(g, 2))
                else:
                    pe.wait_ge(f_pick.sem, f_pick.at(g, 1))
                mm(bank[7][:], w_me[:, js], xmT[:], start=True, stop=True).then_inc(f_me.sem, 1)

            def f_ml_(g, j):
                js = slice(j * P, (j + 1) * P)
                if j < 2:
                    pe.wait_ge(f_hid.sem, f_hid.at(g))
                else:
                    pe.wait_ge(f_mlg.sem, f_mlg.at(g, j - 1))
                mm(bank[4 + j % 2][:], w_ml1[:, js], xmT[:], start=True, stop=True).then_inc(f_ml.sem, 1)

            def f_ce_apply(g):
                pe.wait_ge(n_c.steps.sem, n_c.steps.at(g))
                turn(bank[6], lambda t: ce_rows[:, t, :]).then_inc(f_ce.sem, 1)

            def f_relu_(g, j):
                js = slice(j * P, (j + 1) * P)
                pe.wait_ge(f_cec.sem, f_cec.at(g, 1))
                if j:
                    pe.wait_ge(f_meg.sem, f_meg.at(g, 1))
                mm(bank[6 + j][:], w_f1[:, js], ce_T, start=True, stop=True).then_inc(f_r.sem, 1)

            def f_ce2(g):
                pe.wait_ge(f_relu.sem, f_relu.at(g))
                for t in range(T):
                    ts = slice(t * P, (t + 1) * P)
                    for j in range(2):
                        last = mm(bank[6][:, ts], hid_relu[j][:, ts], w_f2[:, j, :], start=(j == 0), stop=(j == 1))
                last.then_inc(f_ce.sem, 1)

            def f_ce2_apply(g):
                pe.wait_ge(n_c2.steps.sem, n_c2.steps.at(g))
                turn(bank[6], lambda t: ce_rows[:, t, :]).then_inc(f_gT.sem, 1)

            def f_out(g, t):
                ts = slice(t * P, (t + 1) * P)
                if t == 0:
                    pe.wait_ge(f_mlg.sem, f_mlg.at(g))
                    pe.wait_ge(f_meg.sem, f_meg.at(g))
                    pe.wait_ge(f_cec.sem, f_cec.at(g))
                out_b = bank[4 + t]
                for j in range(J1):
                    mm(out_b[:, 0:P], hid_sw[j][:, ts], w_sw2[:, j, :], start=(j == 0), stop=(j == J1 - 1))
                for j in range(2):
                    mm(out_b[:, P:2 * P], hid_me[j][:, ts], w_c2[:, j, :], start=(j == 0), stop=(j == 1))
                mm(out_b[:, 2 * P:3 * P], ce_T[:, ts], w_gen[:], start=True, stop=True)
                for j in range(J1):
                    last = mm(out_b[:, 3 * P:], hid_ml[j][:, ts], w_ml2[:, j, :], start=(j == 0), stop=(j == J1 - 1))
                last.then_inc(f_e.sem, 1)

            plan(pe, {
                "s_w0": s_w0, "s_turn": s_turn, "s_fold1": s_fold1, "s_fold2": s_fold2, "s_fold3": s_fold3, "s_fold4": s_fold4,
                "s_split": s_split,
                "e_turn1": e_turn1, "l_turn2": l_turn2, "l_turn3": l_turn3, "l_route": l_route, "l_ct": l_cT,
                "l_g": l_g_, "l_u": l_u_, "l_c": l_c_, "l_down": l_down_,
                "l_x": l_x, "a_null": a_null, "a_m": a_m, "a_t": a_t, "a_v": a_v,
                "a_scores": a_scores, "a_mix": a_mix_, "a_ot": a_oT_, "a_out": a_out_,
                "f_turn": f_turn, "f_route": f_route, "f_ce": f_ce_, "f_sw": f_sw, "f_me": f_me_, "f_ml": f_ml_,
                "f_cet": f_ce_apply, "f_relu": f_relu_, "f_ce2": f_ce2, "f_ce2t": f_ce2_apply, "f_out": f_out,
            })


def build(nc, inputs):
    arrays, args = {}, {}
    for name, value in inputs.items():
        v = np.ascontiguousarray(value)
        arrays[f"in_{name}"] = v
        args[name] = nc.dram_tensor(f"in_{name}", v.shape, mybir.dt.from_np(v.dtype), kind="ExternalInput").ap()
    out = nc.dram_tensor("out_0", inputs["L0_attn_x"].shape, F32, kind="ExternalOutput").ap()
    program(nc, args, out)
    return arrays


def kernel(**inputs):
    import concourse.bacc as bacc
    from concourse.bass_utils import run_bass_kernel_spmd

    nc = bacc.Bacc("TRN2", target_bir_lowering=False, num_devices=1)
    arrays = build(nc, inputs)
    r = run_bass_kernel_spmd(nc, [arrays], core_ids=[0])
    return r.results[0]["out_0"]
```
